# Optimizing a Trainium2 kernel written in Bass

```python
import numpy as np
import jax
import jax.numpy as jnp

def _softmax(x, axis=-1):
    return jax.nn.softmax(x, axis=axis)
def _gelu(x):
    return jax.nn.gelu(x, approximate=True)
def _silu(x):
    return jax.nn.silu(x)
def _sigmoid(x):
    return jax.nn.sigmoid(x)
def _layernorm(x, axis=-1, eps=1e-5):
    m = jnp.mean(x, axis=axis, keepdims=True)
    v = jnp.var(x, axis=axis, keepdims=True)
    return (x - m) / jnp.sqrt(v + eps)
def _scatter_add(tgt, idx, src, axis=0):
    return tgt.at[idx].add(src)
def _segment_sum(src, seg, n):
    return jax.ops.segment_sum(src, seg, n)

kernel_name = 'mk_conv_seq_d2_conv_nchw512_0b164e'

def setup_inputs(seed: int = 0):
    np.random.seed(seed)
    _w = jnp.asarray
    def _rec_inputs():
        import jax
        import jax.numpy as jnp
        _gk = jax.random.key(seed)
        x = -0.0002928 + 1 * jax.random.normal(jax.random.fold_in(_gk, 1), (8, 512, 32, 32), jnp.float32)
        return x
    x = _rec_inputs()
    def _L0_conv_setup():
        import jax, jax.numpy as jnp
        import numpy as np
        NUM_GROUPS = 32
        NUM_HEADS = 8
        EPS = 1e-05
        RESCALE = 1.0

        def _group_norm(x, gamma, beta):
            B, C, H, W = x.shape
            xg = x.reshape(B, NUM_GROUPS, C // NUM_GROUPS, H, W)
            mu = xg.mean(axis=(2, 3, 4), keepdims=True)
            var = jnp.mean(jnp.square(xg - mu), axis=(2, 3, 4), keepdims=True)
            xn = ((xg - mu) * jax.lax.rsqrt(var + EPS)).reshape(B, C, H, W)
            return xn * gamma[None, :, None, None] + beta[None, :, None, None]

        def _layer_norm(x, gamma, beta):
            mu = x.mean(axis=-1, keepdims=True)
            var = jnp.mean(jnp.square(x - mu), axis=-1, keepdims=True)
            return (x - mu) * jax.lax.rsqrt(var + EPS) * gamma + beta
        key = jax.random.key(seed)
        ks = jax.random.split(key, 12)
        C = 512
        B, H, W = (8, 32, 32)
        s = 1.0 / np.sqrt(C)
        return {'hidden_states': jax.random.normal(ks[0], (B, C, H, W), jnp.float32), 'gn_gamma': jnp.ones((C,), jnp.float32), 'gn_beta': jnp.zeros((C,), jnp.float32), 'wq': jax.random.normal(ks[1], (C, C), jnp.float32) * s, 'bq': jnp.zeros((C,), jnp.float32), 'wk': jax.random.normal(ks[2], (C, C), jnp.float32) * s, 'bk': jnp.zeros((C,), jnp.float32), 'wv': jax.random.normal(ks[3], (C, C), jnp.float32) * s, 'bv': jnp.zeros((C,), jnp.float32), 'wo': jax.random.normal(ks[4], (C, C), jnp.float32) * s, 'bo': jnp.zeros((C,), jnp.float32), 'ln_gamma': jnp.ones((C,), jnp.float32), 'ln_beta': jnp.zeros((C,), jnp.float32)}
    _L0_conv_all = _L0_conv_setup()
    _L0_conv_in = {k: v for k, v in _L0_conv_all.items() if k in ('gn_gamma', 'gn_beta', 'wq', 'bq', 'wk', 'bk', 'wv', 'bv', 'wo', 'bo', 'ln_gamma', 'ln_beta', )}
    del _L0_conv_all

    def _L1_conv_setup():
        import jax, jax.numpy as jnp
        import numpy as np
        B, C, HH, WW = (16, 512, 32, 32)
        NUM_HEADS = 8
        NUM_GROUPS = 32
        EPS = 1e-05
        key = jax.random.key(seed)
        ks = jax.random.split(key, 4)
        x = jax.random.normal(ks[0], (B, C, HH, WW), dtype=jnp.float32)
        gn_scale = jnp.ones((C,), dtype=jnp.float32)
        gn_bias = jnp.zeros((C,), dtype=jnp.float32)
        qkv_w = jax.random.normal(ks[1], (3 * C, C), dtype=jnp.float32) * (1.0 / np.sqrt(C))
        qkv_b = jnp.zeros((3 * C,), dtype=jnp.float32)
        proj_w = jax.random.normal(ks[2], (C, C), dtype=jnp.float32) * (1.0 / np.sqrt(C))
        proj_b = jnp.zeros((C,), dtype=jnp.float32)
        return {'x': x, 'gn_scale': gn_scale, 'gn_bias': gn_bias, 'qkv_w': qkv_w, 'qkv_b': qkv_b, 'proj_w': proj_w, 'proj_b': proj_b}
    _L1_conv_all = _L1_conv_setup()
    _L1_conv_in = {k: v for k, v in _L1_conv_all.items() if k in ('gn_scale', 'gn_bias', 'qkv_w', 'qkv_b', 'proj_w', 'proj_b', )}
    del _L1_conv_all

    return {
        "x": x,
        "L0_conv_gn_gamma": _L0_conv_in["gn_gamma"],
        "L0_conv_gn_beta": _L0_conv_in["gn_beta"],
        "L0_conv_wq": _L0_conv_in["wq"],
        "L0_conv_bq": _L0_conv_in["bq"],
        "L0_conv_wk": _L0_conv_in["wk"],
        "L0_conv_bk": _L0_conv_in["bk"],
        "L0_conv_wv": _L0_conv_in["wv"],
        "L0_conv_bv": _L0_conv_in["bv"],
        "L0_conv_wo": _L0_conv_in["wo"],
        "L0_conv_bo": _L0_conv_in["bo"],
        "L0_conv_ln_gamma": _L0_conv_in["ln_gamma"],
        "L0_conv_ln_beta": _L0_conv_in["ln_beta"],
        "L1_conv_gn_scale": _L1_conv_in["gn_scale"],
        "L1_conv_gn_bias": _L1_conv_in["gn_bias"],
        "L1_conv_qkv_w": _L1_conv_in["qkv_w"],
        "L1_conv_qkv_b": _L1_conv_in["qkv_b"],
        "L1_conv_proj_w": _L1_conv_in["proj_w"],
        "L1_conv_proj_b": _L1_conv_in["proj_b"],
    }

def reference(x, L0_conv_gn_gamma, L0_conv_gn_beta, L0_conv_wq, L0_conv_bq, L0_conv_wk, L0_conv_bk, L0_conv_wv, L0_conv_bv, L0_conv_wo, L0_conv_bo, L0_conv_ln_gamma, L0_conv_ln_beta, L1_conv_gn_scale, L1_conv_gn_bias, L1_conv_qkv_w, L1_conv_qkv_b, L1_conv_proj_w, L1_conv_proj_b):
    import jax
    import jax.numpy as jnp
    def _L0_conv_ref(hidden_states, gn_gamma, gn_beta, wq, bq, wk, bk, wv, bv, wo, bo, ln_gamma, ln_beta):
        import jax, jax.numpy as jnp
        import numpy as np
        NUM_GROUPS = 32
        NUM_HEADS = 8
        EPS = 1e-05
        RESCALE = 1.0

        def _group_norm(x, gamma, beta):
            B, C, H, W = x.shape
            xg = x.reshape(B, NUM_GROUPS, C // NUM_GROUPS, H, W)
            mu = xg.mean(axis=(2, 3, 4), keepdims=True)
            var = jnp.mean(jnp.square(xg - mu), axis=(2, 3, 4), keepdims=True)
            xn = ((xg - mu) * jax.lax.rsqrt(var + EPS)).reshape(B, C, H, W)
            return xn * gamma[None, :, None, None] + beta[None, :, None, None]

        def _layer_norm(x, gamma, beta):
            mu = x.mean(axis=-1, keepdims=True)
            var = jnp.mean(jnp.square(x - mu), axis=-1, keepdims=True)
            return (x - mu) * jax.lax.rsqrt(var + EPS) * gamma + beta
        residual = hidden_states
        B, C, H, W = hidden_states.shape
        x = _group_norm(hidden_states, gn_gamma, gn_beta)
        x = x.reshape(B, C, H * W).transpose(0, 2, 1)
        q = x @ wq.T + bq
        k = x @ wk.T + bk
        v = x @ wv.T + bv
        T = H * W
        dh = C // NUM_HEADS
        q = q.reshape(B, T, NUM_HEADS, dh).transpose(0, 2, 1, 3)
        k = k.reshape(B, T, NUM_HEADS, dh).transpose(0, 2, 1, 3)
        v = v.reshape(B, T, NUM_HEADS, dh).transpose(0, 2, 1, 3)
        scale = 1.0 / np.sqrt(np.sqrt(dh))
        scores = jnp.einsum('bhid,bhjd->bhij', q * scale, k)
        probs = jax.nn.softmax(scores.astype(jnp.float32), axis=-1).astype(scores.dtype)
        ctx = jnp.einsum('bhij,bhjd->bhid', probs, v)
        ctx = ctx.transpose(0, 2, 1, 3).reshape(B, T, C)
        out = _layer_norm(ctx @ wo.T + bo, ln_gamma, ln_beta)
        out = out.transpose(0, 2, 1).reshape(B, C, H, W)
        return (out + residual) / RESCALE

    def _L1_conv_ref(x, gn_scale, gn_bias, qkv_w, qkv_b, proj_w, proj_b):
        import jax, jax.numpy as jnp
        import numpy as np
        B, C, HH, WW = (16, 512, 32, 32)
        NUM_HEADS = 8
        NUM_GROUPS = 32
        EPS = 1e-05
        b, c, h, w = x.shape
        t = h * w
        nh = NUM_HEADS
        d = c // nh
        xf = x.reshape(b, c, t)
        xg = xf.reshape(b, NUM_GROUPS, c // NUM_GROUPS * t)
        mu = jnp.mean(xg, axis=-1, keepdims=True)
        var = jnp.var(xg, axis=-1, keepdims=True)
        xn = ((xg - mu) * jax.lax.rsqrt(var + EPS)).reshape(b, c, t)
        xn = xn * gn_scale[:, None] + gn_bias[:, None]
        qkv = jnp.einsum('oc,bct->bot', qkv_w, xn) + qkv_b[:, None]
        qkv = qkv.reshape(b, 3, nh, d, t)
        q, k, v = (qkv[:, 0], qkv[:, 1], qkv[:, 2])
        scale = 1.0 / jnp.sqrt(jnp.asarray(d, x.dtype))
        logits = jnp.einsum('bhdt,bhds->bhts', q, k) * scale
        probs = jax.nn.softmax(logits, axis=-1)
        attn = jnp.einsum('bhts,bhds->bhdt', probs, v)
        hout = attn.reshape(b, c, t)
        hout = jnp.einsum('oc,bct->bot', proj_w, hout) + proj_b[:, None]
        return (hout + xf).reshape(b, c, h, w)

    def _gn(v, G=32, eps=1e-5):
        B_, C_, H_, W_ = v.shape
        g = v.reshape(B_, G, C_ // G, H_, W_)
        m = jnp.mean(g, axis=(2, 3, 4), keepdims=True)
        s = jnp.var(g, axis=(2, 3, 4), keepdims=True)
        return ((g - m) / jnp.sqrt(s + eps)).reshape(v.shape)

    def _ln_c(v, eps=1e-6):
        m = jnp.mean(v, axis=1, keepdims=True)
        s = jnp.var(v, axis=1, keepdims=True)
        return (v - m) / jnp.sqrt(s + eps)

    def _ln_t(v, eps=1e-5):
        m = jnp.mean(v, axis=-1, keepdims=True)
        s = jnp.var(v, axis=-1, keepdims=True)
        return (v - m) / jnp.sqrt(s + eps)

    def _to_tokens(v):
        B_, C_, H_, W_ = v.shape
        return v.reshape(B_, C_, H_ * W_).transpose(0, 2, 1)
    def _from_tokens(t, like):
        B_, C_, H_, W_ = like.shape
        return t.transpose(0, 2, 1).reshape(B_, C_, H_, W_)

    x = _L0_conv_ref(x, L0_conv_gn_gamma, L0_conv_gn_beta, L0_conv_wq, L0_conv_bq, L0_conv_wk, L0_conv_bk, L0_conv_wv, L0_conv_bv, L0_conv_wo, L0_conv_bo, L0_conv_ln_gamma, L0_conv_ln_beta)
    x = _L1_conv_ref(x, L1_conv_gn_scale, L1_conv_gn_bias, L1_conv_qkv_w, L1_conv_qkv_b, L1_conv_proj_w, L1_conv_proj_b)
    return x


_drawn_inputs = setup_inputs


def setup_inputs(seed=0):
    import zlib

    import numpy as np

    out = dict(_drawn_inputs(seed))
    spreads = {'L0_conv_gn_gamma': (1.0, 0.2),
     'L0_conv_gn_beta': (0.0, 0.1),
     'L0_conv_bq': (0.0, 0.1),
     'L0_conv_bk': (0.0, 0.1),
     'L0_conv_bv': (0.0, 0.1),
     'L0_conv_bo': (0.0, 0.1),
     'L0_conv_ln_gamma': (1.0, 0.2),
     'L0_conv_ln_beta': (0.0, 0.1),
     'L1_conv_gn_scale': (1.0, 0.2),
     'L1_conv_gn_bias': (0.0, 0.1),
     'L1_conv_qkv_b': (0.0, 0.1),
     'L1_conv_proj_b': (0.0, 0.1)}
    factors = {}
    for name, (base, spread) in spreads.items():
        noise = np.random.default_rng([zlib.crc32(name.encode()), seed]).standard_normal(out[name].shape)
        drawn = base * np.exp(spread * noise) if base else spread * noise
        out[name] = jnp.asarray(drawn.astype(out[name].dtype))
    for name, factor in factors.items():
        out[name] = (out[name] * factor).astype(out[name].dtype)
    return out
```

```python
from contextlib import ExitStack

import concourse.bass as bass
from concourse import mybir

F32 = mybir.dt.float32
F32R = mybir.dt.float32r
ALU = mybir.AluOpType
ACT = mybir.ActivationFunctionType
AX_X = mybir.AxisListType.X

P = 128
B, C, T = 8, 512, 1024
HEADS, D = 8, 64
GROUPS = 32
EPS = 1e-5
CT = C // P
PAIRS = HEADS // 2
HALF = T // 2
UNITS = 2 * PAIRS
KT = T // P
STEPS = KT
RING = 4
QUERY_TILES = HALF // P
OUT_TILES = 8
LAYERS = 2
PARTS = 4
QUERY_SCALE = (float(D) ** -0.25, float(D) ** -0.5)


class Count:

    def __init__(self, sem, per_image, ahead=0, by=1):
        self.sem, self.per_image, self.ahead, self.by = sem, per_image, ahead, by

    def at(self, layer, b, k):
        return (layer * (B * self.per_image + self.ahead) + k) * self.by + 1 + b * (self.per_image * self.by)


def attention_blocks(nc, x, out, middle, weights, wv_in, wo_in, columns, rows, constants):
    with ExitStack() as ctx_:
        def sb(name, shape, dt=F32):
            return ctx_.enter_context(nc.sbuf_tensor(name, shape, dt))

        def psum(name, shape):
            return ctx_.enter_context(nc.psum_tensor(name, shape, F32))

        def sem(name):
            return ctx_.enter_context(nc.semaphore(name))

        counts = []

        def count(name, per_image, ahead=0, by=1):
            counts.append(Count(sem(name), per_image, ahead, by))
            return counts[-1]

        consts = sb("consts", [P, 2 * P + D])
        identity, group_mean, ones = consts[:, 0:P], consts[:, P:2 * P], consts[:, 2 * P:2 * P + D]
        cols = sb("cols", [P, 6, CT])
        gamma, beta, bq, bk = (cols[:, i, :] for i in range(4))
        bias_rows = sb("bias_rows", [P, 2, C])
        bqs = sb("bqs", [P, CT])
        wv = sb("wv", [P, 2, CT, C], F32R)
        wo = sb("wo", [P, CT, C])
        wqk_raw = sb("wqk_raw", [P, 2, CT * P])
        wqk = sb("wqk", [P, 2, 2, 2, CT * P], F32R)
        x_in = sb("x_in", [P, 2, T])
        xn = sb("xn", [P, 2, CT, T], F32R)
        q_both = sb("q_both", [P, 2, 2, HALF], F32R)
        q_low = sb("q_low", [P, 2, 2, HALF], F32R)
        k_parts = sb("k_parts", [P, 2, 2, T], F32R)
        k_ones = sb("k_ones", [P, 2, 2, T], F32R)
        v = sb("v", [P, KT, C])
        e = sb("e", [P, RING, 2, HALF])
        e_sum = sb("e_sum", [P, 2, HALF])
        inv_sum = sb("inv_sum", [P, HALF])
        neg_max = sb("neg_max", [P, QUERY_TILES, P])
        heads_out = sb("heads_out", [P, CT, T])
        x_res = sb("x_res", [P, 2, HALF])
        y_out = sb("y_out", [P, 2, HALF])
        y_tok = sb("y_tok", [P, 2, C])
        bn = sb("bn", [P, CT, 3 * PARTS])
        part_means, part_squares = (bn[:, :, :].rearrange("p c (g k) -> p (c g) k", k=3)[:, :, i] for i in (1, 2))
        g_mean = sb("g_mean", [P, CT])
        g_dev = sb("g_dev", [P, CT * PARTS])
        g_sq = sb("g_sq", [P, CT * PARTS])
        g_exp = sb("g_exp", [P, CT * PARTS])
        g_sum = sb("g_sum", [P, CT])
        g_var = sb("g_var", [P, CT])
        g_rstd = sb("g_rstd", [P, CT])
        g_scale = sb("g_scale", [P, CT])
        g_tmp = sb("g_tmp", [P, CT])
        g_shift = sb("g_shift", [P, CT])
        minus_half = sb("minus_half", [P, CT])
        ln_bn = sb("ln_bn", [P, 2, 6])
        ln_sums = sb("ln_sums", [P, 2, 2])
        ln_diff = sb("ln_diff", [P, 2, 1])
        ln_mean = sb("ln_mean", [P, 2, 1])
        ln_within = sb("ln_within", [P, 2, 1])
        ln_between = sb("ln_between", [P, 2, 1])
        ln_var = sb("ln_var", [P, 2, 1])
        ln_rstd = sb("ln_rstd", [P, 2, 1])

        scores_ps = [psum(f"scores_ps{i}", [P, 2, HALF]) for i in range(2)]
        max_ps = psum("max_ps", [P, 2, HALF])
        acc_ps = psum("acc_ps", [P, HALF])
        gen_ps = psum("gen_ps", [P, HALF])

        k_acc = count("k_acc", 2 * PAIRS)
        q_acc = count("q_acc", UNITS)
        v_acc = count("v_acc", KT)
        max_acc = count("max_acc", 8 * UNITS)
        mt_acc = count("mt_acc", UNITS)
        s_acc = count("s_acc", STEPS * UNITS)
        pv_acc = count("pv_acc", 4 * UNITS)
        l_acc = count("l_acc", UNITS)
        o_acc = count("o_acc", OUT_TILES)
        gn_mean_acc = count("gn_mean_acc", 1, 1)
        gn_var_acc = count("gn_var_acc", 1, 1)
        zt_acc = count("zt_acc", OUT_TILES)
        w_high = count("w_high", PAIRS, 2)
        k_high = count("k_high", 2 * PAIRS)
        q_high = count("q_high", UNITS)
        m_high = count("m_high", UNITS)
        exp_done = count("exp_done", STEPS * UNITS)
        x_high = count("x_high", CT, CT)
        ctx_raw = count("ctx_raw", UNITS)
        ln_done = count("ln_done", OUT_TILES)
        wv_high = sem("wv_high")
        w_low = count("w_low", PAIRS, 2)
        k_low_done = count("k_low_done", 2 * PAIRS)
        q_low_done = count("q_low_done", UNITS)
        m_low = count("m_low", UNITS)
        max_done = count("max_done", 8 * UNITS)
        v_done = count("v_done", KT)
        inv_done = count("inv_done", UNITS)
        ctx_done = count("ctx_done", UNITS)
        bn_done = count("bn_done", CT, CT)
        gn_step = count("gn_step", 6, 6)
        x_norm = count("x_norm", CT, CT)
        x_low = count("x_low", CT, CT)
        y_done = count("y_done", OUT_TILES)
        ln_stat = count("ln_stat", 4 * OUT_TILES)
        z_done = count("z_done", OUT_TILES)
        out_done = count("out_done", OUT_TILES)
        prep_done = sem("prep_done")
        zeroed = sem("zeroed")
        sum_part = count("sum_part", 6 * UNITS)
        sum_done = count("sum_done", STEPS * UNITS)
        gn_coef = count("gn_coef", 4, 4)
        ln_pow = count("ln_pow", OUT_TILES)
        setup_in = sem("setup_in")
        layer_in = sem("layer_in")
        wv_in_sem = sem("wv_in_sem")
        w_in = count("w_in", PAIRS, 2, by=32)
        x_loaded = [count(f"x_loaded{i}", CT, CT, by=16) for i in range(2)]
        res_in = [count(f"res_in{i}", OUT_TILES // 2, by=16) for i in range(2)]
        stored = [count(f"stored{i}", OUT_TILES // 2, by=16) for i in range(2)]

        block = ctx_.enter_context(nc.Block())
        LOW, TOP = slice(0, D), slice(D, P)
        OWN = (LOW, TOP)
        OTHER = (TOP, LOW)
        MAX_ROWS = ((D, D + 32), (0, 32))

        def columns_of(tile, n=P):
            return slice(tile * n, (tile + 1) * n)

        @block.sync
        def _(sp):
            sp.dma_start(consts[:], constants).then_inc(setup_in, 16)
            for layer in range(LAYERS):
                source = x if layer == 0 else middle
                target = middle if layer == 0 else out

                def load_stats(gi_b, img, ct, layer=layer, source=source):
                    if ct < 2:
                        sp.wait_ge(x_low.sem, x_low.at(layer, gi_b, 0))
                    else:
                        sp.wait_ge(bn_done.sem, bn_done.at(layer, gi_b, ct - 1))
                    sp.dma_start(x_in[:, ct % 2, :], source[img, columns_of(ct), :])\
                        .then_inc(x_loaded[ct % 2].sem, 16)

                def load_norm(gi_b, img, ct, layer=layer, source=source):
                    if ct < 2:
                        sp.wait_ge(bn_done.sem, bn_done.at(layer, gi_b, ct + 3))
                    else:
                        sp.wait_ge(x_low.sem, x_low.at(layer, gi_b, ct - 1))
                    sp.dma_start(x_in[:, ct % 2, :], source[img, columns_of(ct), :])\
                        .then_inc(x_loaded[ct % 2].sem, 16)

                def load_wqk(b, k, layer=layer):
                    sp.wait_ge(w_high.sem, w_high.at(layer, b, k))
                    sp.wait_ge(w_low.sem, w_low.at(layer, b, k))
                    for which in range(2):
                        sp.dma_start(wqk_raw[:, which, :], weights[layer][k % PAIRS, which]).then_inc(w_in.sem, 16)

                if layer:
                    for ring in range(2):
                        sp.wait_ge(stored[ring].sem, stored[ring].at(layer, 0, 0))
                    sp.wait_ge(x_low.sem, x_low.at(layer, 0, 0))
                sp.dma_start(cols[:, :, :], columns[layer]).then_inc(layer_in, 16)
                for i in range(2):
                    sp.dma_start(bias_rows[:, i, :], rows[layer][i:i + 1, :].broadcast_to([P, C])).then_inc(layer_in, 16)
                sp.dma_start(wo[:, :, :], wo_in[layer]).then_inc(layer_in, 16)
                for ct in range(CT):
                    load_stats(0, 0, ct)
                load_wqk(0, 0)
                load_wqk(0, 1)
                for ct in range(CT):
                    load_norm(0, 0, ct)
                sp.dma_start(v[:, 0:CT, :], wv_in[layer]).then_inc(wv_in_sem, 16)

                with sp.Fori(0, B) as b:
                    nxt = (b + 1) % B
                    load_wqk(b, 2)
                    load_stats(b + 1, nxt, 0)
                    load_stats(b + 1, nxt, 1)
                    load_stats(b + 1, nxt, 2)
                    load_wqk(b, 3)
                    load_stats(b + 1, nxt, 3)
                    load_wqk(b, 4)
                    load_norm(b + 1, nxt, 0)
                    load_norm(b + 1, nxt, 1)
                    load_wqk(b, 5)

                    def load_res(n):
                        sp.wait_ge(out_done.sem, out_done.at(layer, b, max(n - 1, 0)))
                        if layer == 0:
                            src = source[b].rearrange("(c p) t -> p c t", p=P)[:, :, columns_of(n)]
                            dst = x_res[:, n % 2, :].rearrange("p (c t) -> p c t", c=CT)
                        else:
                            src = source[b, columns_of(n % CT), columns_of(n // CT, HALF)]
                            dst = x_res[:, n % 2, :]
                        sp.dma_start(dst, src).then_inc(res_in[n % 2].sem, 16)

                    load_res(0)
                    load_res(1)
                    load_norm(b + 1, nxt, 2)
                    load_norm(b + 1, nxt, 3)
                    for n in range(OUT_TILES):
                        sp.wait_ge(out_done.sem, out_done.at(layer, b, n + 1))
                        if layer == 0:
                            dst = target[b].rearrange("(c p) t -> p c t", p=P)[:, :, columns_of(n)]
                            src = y_out[:, n % 2, :].rearrange("p (c t) -> p c t", c=CT)
                        else:
                            dst = target[b, columns_of(n % CT), columns_of(n // CT, HALF)]
                            src = y_out[:, n % 2, :]
                        sp.dma_start(dst, src).then_inc(stored[n % 2].sem, 16)
                        if n + 2 < OUT_TILES:
                            load_res(n + 2)
            for ring in range(2):
                sp.wait_ge(stored[ring].sem, stored[ring].at(LAYERS, 0, 0))

        @block.tensor
        def _(pe):
            pe.wait_ge(setup_in, 16)
            pe.wait_ge(zeroed, 4)
            for layer in range(LAYERS):
                gen_reader = []

                def fill_gen(*readers):
                    for counter, value in gen_reader:
                        pe.wait_ge(counter.sem, value)
                    gen_reader[:] = readers

                def group_means(b, layer=layer):
                    pe.wait_ge(bn_done.sem, bn_done.at(layer, b, CT))
                    fill_gen((gn_step, gn_step.at(layer, b, 1)))
                    pe.matmul(gen_ps[:, 0:CT * PARTS], group_mean, part_means, start=True, stop=True)\
                        .then_inc(gn_mean_acc.sem, 1)

                def group_vars(b, layer=layer):
                    pe.wait_ge(gn_step.sem, gn_step.at(layer, b, 4))
                    fill_gen((gn_step, gn_step.at(layer, b, 5)))
                    pe.matmul(gen_ps[:, 0:CT * PARTS], group_mean, g_exp[:, :], start=True, stop=True)\
                        .then_inc(gn_var_acc.sem, 1)

                def project(dst, which, pair, half, b):
                    pe.wait_ge(w_high.sem, w_high.at(layer, b, pair + 1))
                    pe.wait_ge(w_low.sem, w_low.at(layer, b, pair + 1))
                    n = 0
                    for kt in range(CT):
                        for w_part, x_part in ((0, 0), (0, 1), (1, 0)):
                            mm = pe.matmul(dst, wqk[:, pair % 2, which, w_part, columns_of(kt)],
                                           xn[:, x_part, kt, columns_of(half, HALF)],
                                           start=n == 0, stop=n == 3 * CT - 1)
                            n += 1
                    return mm

                def k_tile(b, pair, half):
                    n = 2 * pair + half
                    fill_gen((k_high, k_high.at(layer, b, n + 1)), (k_low_done, k_low_done.at(layer, b, n + 1)))
                    project(gen_ps[:, :], 1, pair, half, b).then_inc(k_acc.sem, 1)

                def q_tile(b, u):
                    fill_gen((q_high, q_high.at(layer, b, u + 1)), (q_low_done, q_low_done.at(layer, b, u + 1)))
                    project(gen_ps[:, :], 0, u // 2, u % 2, b).then_inc(q_acc.sem, 1)

                def v_tile(b, jt):
                    if jt % 2 == 0:
                        fill_gen((v_done, v_done.at(layer, b, jt + 1)))
                        dst = gen_ps[:, :]
                    else:
                        if jt == 1:
                            pe.wait_ge(ctx_raw.sem, ctx_raw.at(layer, b, 0))
                        else:
                            pe.wait_ge(v_done.sem, v_done.at(layer, b, jt - 1))
                        dst = acc_ps[:, :]
                    n = 0
                    for kt in range(CT):
                        for x_part, w_part in ((0, 0), (0, 1), (1, 0)):
                            mm = pe.matmul(dst, xn[:, x_part, kt, columns_of(jt)], wv[:, w_part, kt, :],
                                           start=n == 0, stop=n == 3 * CT - 1)
                            n += 1
                    mm.then_inc(v_acc.sem, 1)

                def max_step(b, u, m):
                    it, head = m // 2, m % 2
                    if m == 0:
                        pe.wait_ge(q_high.sem, q_high.at(layer, b, u + 1))
                        pe.wait_ge(k_high.sem, k_high.at(layer, b, 2 * (u // 2) + 2))
                        pe.wait_ge(k_low_done.sem, k_low_done.at(layer, b, 2 * (u // 2) + 2))
                    pe.wait_ge(max_done.sem, max_done.at(layer, b, 8 * u + m))
                    for half in range(2):
                        mm = pe.matmul(max_ps[:, half, :], q_both[:, u % 2, head, columns_of(it)],
                                       k_parts[:, u // 2 % 2, head, columns_of(half, HALF)], start=True, stop=True)
                    mm.then_inc(max_acc.sem, 1)

                def max_rows(b, u):
                    pe.wait_ge(max_done.sem, max_done.at(layer, b, 8 * (u + 1)))
                    fill_gen((m_high, m_high.at(layer, b, u + 1)), (m_low, m_low.at(layer, b, u + 1)))
                    for it in range(QUERY_TILES):
                        mm = pe.transpose(gen_ps[:, columns_of(it)], neg_max[:, it, :], identity)
                    mm.then_inc(mt_acc.sem, 1)

                def score_step(b, u, s):
                    head, ring, n = s % 2, u % 2, STEPS * u + s
                    if s == 0:
                        pe.wait_ge(m_high.sem, m_high.at(layer, b, u + 1))
                        pe.wait_ge(m_low.sem, m_low.at(layer, b, u + 1))
                        pe.wait_ge(q_low_done.sem, q_low_done.at(layer, b, u + 1))
                    pe.wait_ge(exp_done.sem, exp_done.at(layer, b, max(n - 1, 0)))
                    for i in range(2):
                        keys = columns_of(s // 2 * 2 + i)
                        pe.matmul(scores_ps[s % 2][:, i, :], k_parts[:, u // 2 % 2, head, keys],
                                  q_both[:, ring, head, :], start=True, stop=False)
                        mm = pe.matmul(scores_ps[s % 2][:, i, :], k_ones[:, u // 2 % 2, head, keys],
                                       q_low[:, ring, head, :], start=False, stop=True)
                    mm.then_inc(s_acc.sem, 1)

                def value_step(b, u, j2):
                    pe.wait_ge(exp_done.sem, exp_done.at(layer, b, STEPS * u + 2 * j2 + 2))
                    if j2 == 0:
                        if u == 0:
                            pe.wait_ge(v_done.sem, v_done.at(layer, b, KT))
                        else:
                            pe.wait_ge(ctx_raw.sem, ctx_raw.at(layer, b, u))
                    for i in range(2):
                        jt = 2 * j2 + i
                        for head in range(2):
                            at = (2 * (u // 2) + head) * D
                            mm = pe.matmul(acc_ps[OWN[head], :], v[:, jt, at:at + D],
                                           e[:, (2 * j2 + head) % RING, i, :], start=jt == 0, stop=jt == KT - 1)
                    mm.then_inc(pv_acc.sem, 1)

                def sum_step(b, u):
                    pe.wait_ge(sum_done.sem, sum_done.at(layer, b, STEPS * (u + 1)))
                    fill_gen((inv_done, inv_done.at(layer, b, u + 1)))
                    for head in range(2):
                        mm = pe.matmul(gen_ps[OWN[head], :], ones, e_sum[:, head, :], start=True, stop=True)
                    mm.then_inc(l_acc.sem, 1)

                def out_tile(b, n):
                    pe.wait_ge(ctx_done.sem, ctx_done.at(layer, b, UNITS - 1 + n // 4))
                    if n < 2:
                        pe.wait_ge(max_done.sem, max_done.at(layer, b, 8 * UNITS))
                    else:
                        reader = y_done if layer == 0 else out_done
                        pe.wait_ge(reader.sem, reader.at(layer, b, n - 1))
                    for kt in range(CT):
                        if layer == 0:
                            lhs, rhs = heads_out[:, kt, columns_of(n)], wo[:, kt, :]
                        else:
                            lhs, rhs = wo[:, kt, columns_of(n % CT)], heads_out[:, kt, columns_of(n // CT, HALF)]
                        mm = pe.matmul(max_ps[:, n % 2, :], lhs, rhs, start=kt == 0, stop=kt == CT - 1)
                    mm.then_inc(o_acc.sem, 1)

                def token_turn(b, n):
                    pe.wait_ge(z_done.sem, z_done.at(layer, b, n + 1))
                    fill_gen((ln_done, ln_done.at(layer, b, n + 1)))
                    for ct in range(CT):
                        mm = pe.transpose(gen_ps[:, columns_of(ct)], y_tok[:, n % 2, columns_of(ct)], identity)
                    mm.then_inc(zt_acc.sem, 1)

                def out_step(b, n):
                    if n < OUT_TILES:
                        out_tile(b, n)
                    if layer == 0 and n >= 2:
                        token_turn(b, n - 2)

                if layer:
                    gen_reader[:] = [(ln_done, ln_done.at(1, 0, 0)), (inv_done, inv_done.at(1, 0, 0))]
                group_means(0)
                group_vars(0)
                pe.wait_ge(layer_in, 64 * (layer + 1))
                pe.wait_ge(prep_done, 2 * (layer + 1))
                pe.wait_ge(wv_high, layer + 1)

                with pe.Fori(0, B) as b:
                    pe.wait_ge(x_high.sem, x_high.at(layer, b, CT))
                    pe.wait_ge(x_low.sem, x_low.at(layer, b, CT))
                    gen_reader[:] = [(gn_step, gn_step.at(layer, b, 6)),
                                     (inv_done, inv_done.at(layer, b, 0))]
                    if layer == 0:
                        gen_reader.append((ln_done, ln_done.at(layer, b, 0)))
                    k_tile(b, 0, 0)
                    k_tile(b, 0, 1)
                    q_tile(b, 0)
                    last_out = y_done if layer == 0 else out_done
                    pe.wait_ge(last_out.sem, last_out.at(layer, b, 0))
                    for jt in range(KT):
                        v_tile(b, jt)
                        max_step(b, 0, jt)
                    max_rows(b, 0)
                    for u in range(UNITS):
                        pair, half = u // 2, u % 2
                        for s in range(STEPS):
                            score_step(b, u, s)
                            if u + 1 < UNITS:
                                if half == 1 and s < 2:
                                    k_tile(b, pair + 1, s)
                                if s == (2 if half else 0):
                                    q_tile(b, u + 1)
                            if s == 3 and u > 0:
                                sum_step(b, u - 1)
                            if u + 1 < UNITS and 3 <= s < 7:
                                max_step(b, u + 1, 2 * (s - 3))
                            if s == 4:
                                value_step(b, u, 0)
                            if s == 5:
                                value_step(b, u, 1)
                            if u + 1 < UNITS and 3 <= s < 7:
                                max_step(b, u + 1, 2 * (s - 3) + 1)
                            if s == 7:
                                value_step(b, u, 2)
                            if (u, s) == (4, 4):
                                group_means(b + 1)
                            if (u, s) == (5, 5):
                                group_vars(b + 1)
                            if u == UNITS - 1 and s >= 5:
                                out_step(b, s - 5)
                        if u + 1 < UNITS:
                            max_rows(b, u + 1)
                        value_step(b, u, 3)
                    out_step(b, 3)
                    sum_step(b, UNITS - 1)
                    for n in range(4, OUT_TILES + 2):
                        out_step(b, n)

        @block.scalar
        def _(act):
            act.wait_ge(zeroed, 4)
            for layer in range(LAYERS):
                def split_w(b, k, layer=layer):
                    act.wait_ge(w_in.sem, w_in.at(layer, b, k + 1))
                    if k >= 2:
                        act.wait_ge(q_acc.sem, q_acc.at(layer, b, 2 * (k - 1)))
                    else:
                        act.wait_ge(q_acc.sem, q_acc.at(layer, b, 0))
                    nc.scalar.activation(wqk[:, k % 2, 0, 0, :], wqk_raw[:, 0, :], ACT.Copy, scale=QUERY_SCALE[layer])
                    nc.scalar.activation(wqk[:, k % 2, 1, 0, :], wqk_raw[:, 1, :], ACT.Copy).then_inc(w_high.sem, 1)

                def split_x(b, ct, layer=layer):
                    act.wait_ge(x_norm.sem, x_norm.at(layer, b, ct + 1))
                    nc.scalar.activation(xn[:, 0, ct, :], x_in[:, ct % 2, :], ACT.Copy).then_inc(x_high.sem, 1)

                def split_k(b, pair, half):
                    n, ring = 2 * pair + half, pair % 2
                    act.wait_ge(k_acc.sem, k_acc.at(layer, b, n + 1))
                    act.wait_ge(s_acc.sem, s_acc.at(layer, b, max(2 * STEPS * (pair - 1), 0)))
                    for dst in (k_parts, k_ones):
                        for head in range(2):
                            own = OWN[head]
                            op = nc.scalar.activation(dst[own, ring, head, columns_of(half, HALF)], gen_ps[own, :],
                                                      ACT.Identity, bias=bk[own, pair:pair + 1])
                    op.then_inc(k_high.sem, 1)

                def split_q(b, u):
                    ring, pair = u % 2, u // 2
                    act.wait_ge(q_acc.sem, q_acc.at(layer, b, u + 1))
                    act.wait_ge(s_acc.sem, s_acc.at(layer, b, max(STEPS * (u - 1), 0)))
                    for head in range(2):
                        own = OWN[head]
                        for place in (own, OTHER[head]):
                            op = nc.scalar.activation(q_both[place, ring, head, :], gen_ps[own, :],
                                                      ACT.Identity, bias=bqs[own, pair:pair + 1])
                    op.then_inc(q_high.sem, 1)

                def split_max(b, u):
                    act.wait_ge(mt_acc.sem, mt_acc.at(layer, b, u + 1))
                    act.wait_ge(s_acc.sem, s_acc.at(layer, b, max(STEPS * (u - 1), 0)))
                    for head in range(2):
                        row = MAX_ROWS[head][0]
                        op = nc.scalar.activation(q_low[row:row + 1, u % 2, head, :], gen_ps[row:row + 1, :], ACT.Copy)
                    op.then_inc(m_high.sem, 1)

                def exp_step(b, u, s):
                    n = STEPS * u + s
                    act.wait_ge(s_acc.sem, s_acc.at(layer, b, n + 1))
                    last = n - RING
                    act.wait_ge(pv_acc.sem, pv_acc.at(layer, b, 4 * (last // STEPS) + last % STEPS // 2 + 1 if last >= 0 else 0))
                    act.wait_ge(sum_done.sem, sum_done.at(layer, b, max(last + 1, 0)))
                    nc.scalar.activation(e[:, s % RING, :, :], scores_ps[s % 2][:, :, :], ACT.Exp)\
                        .then_inc(exp_done.sem, 1)

                def take_context(b, u):
                    act.wait_ge(pv_acc.sem, pv_acc.at(layer, b, 4 * (u + 1)))
                    if u < 2:
                        act.wait_ge(o_acc.sem, o_acc.at(layer, b, 0))
                    nc.scalar.activation(heads_out[:, u // 2, columns_of(u % 2, HALF)], acc_ps[:, :], ACT.Copy)\
                        .then_inc(ctx_raw.sem, 1)

                def ln_affine(b, n):
                    act.wait_ge(zt_acc.sem, zt_acc.at(layer, b, n + 1))
                    act.wait_ge(stored[n % 2].sem, stored[n % 2].at(layer, b, n // 2))
                    for ct in range(CT):
                        op = nc.scalar.activation(y_out[:, n % 2, columns_of(ct)], gen_ps[:, columns_of(ct)],
                                                  ACT.Identity, bias=cols[:, 5, ct:ct + 1], scale=cols[:, 4, ct:ct + 1])
                    op.then_inc(ln_done.sem, 1)

                def out_step(b, n):
                    if layer == 0 and n >= 2:
                        ln_affine(b, n - 2)

                split_w(0, 0)
                split_w(0, 1)
                for ct in range(CT):
                    split_x(0, ct)
                act.wait_ge(wv_in_sem, 16 * (layer + 1))
                nc.scalar.activation(wv[:, 0, :, :], v[:, 0:CT, :], ACT.Copy).then_inc(wv_high, 1)
                act.wait_ge(prep_done, 2 * layer + 1)

                with act.Fori(0, B) as b:
                    split_k(b, 0, 0)
                    split_k(b, 0, 1)
                    split_q(b, 0)
                    split_max(b, 0)
                    for u in range(UNITS):
                        pair, half = u // 2, u % 2
                        for s in range(STEPS):
                            exp_step(b, u, s)
                            if u + 1 < UNITS:
                                if half == 1 and s < 2:
                                    split_k(b, pair + 1, s)
                                if s == (2 if half else 0):
                                    split_q(b, u + 1)
                            if s == 6 and u in (1, 3, 5):
                                split_w(b, 2 + u // 2)
                            if u == UNITS - 1:
                                if s < CT:
                                    split_x(b + 1, s)
                                if s == 4:
                                    split_w(b, 5)
                                if s >= 5:
                                    out_step(b, s - 5)
                        if u + 1 < UNITS:
                            split_max(b, u + 1)
                        take_context(b, u)
                    for n in range(3, OUT_TILES + 2):
                        out_step(b, n)

        @block.vector
        def _(dve):
            dve.wait_ge(zeroed, 4)

            for layer in range(LAYERS):
                def split_w(b, k, layer=layer):
                    dve.wait_ge(w_high.sem, w_high.at(layer, b, k + 1))
                    nc.vector.scalar_tensor_tensor(out=wqk[:, k % 2, 0, 1, :], in0=wqk_raw[:, 0, :], scalar=QUERY_SCALE[layer],
                                                   in1=wqk[:, k % 2, 0, 0, :].bitcast(F32), op0=ALU.mult, op1=ALU.subtract)
                    nc.vector.tensor_tensor(wqk[:, k % 2, 1, 1, :], wqk_raw[:, 1, :],
                                            wqk[:, k % 2, 1, 0, :].bitcast(F32), ALU.subtract).then_inc(w_low.sem, 1)

                def image_stats(b, ct, layer=layer):
                    dve.wait_ge(x_loaded[ct % 2].sem, x_loaded[ct % 2].at(layer, b, ct // 2 + 1))
                    for i in range(2):
                        op = nc.vector.bn_stats(bn[:, ct, 6 * i:6 * i + 6], x_in[:, ct % 2, columns_of(i, HALF)])
                    op.then_inc(bn_done.sem, 1)

                def group_deviation(b, layer=layer):
                    step = lambda k: dve.wait_ge(gn_step.sem, gn_step.at(layer, b, k))
                    dve.wait_ge(gn_mean_acc.sem, gn_mean_acc.at(layer, b, 1))
                    dve.wait_ge(gn_coef.sem, gn_coef.at(layer, b, 0))
                    nc.vector.tensor_reduce(g_mean[:, :], gen_ps[:, 0:CT * PARTS].rearrange("p (c g) -> p c g", g=PARTS),
                                            AX_X, ALU.add).then_inc(gn_step.sem, 1)
                    step(1)
                    for ct in range(CT):
                        op = nc.vector.tensor_scalar(g_dev[:, PARTS * ct:PARTS * ct + PARTS],
                                                     part_means[:, PARTS * ct:PARTS * ct + PARTS],
                                                     g_mean[:, ct:ct + 1], None, ALU.subtract)
                    op.then_inc(gn_step.sem, 1)
                    step(2)
                    nc.vector.tensor_tensor(g_sq[:, :], g_dev[:, :], g_dev[:, :], ALU.mult).then_inc(gn_step.sem, 1)
                    step(3)
                    nc.vector.scalar_tensor_tensor(out=g_exp[:, :], in0=part_squares, scalar=float(PARTS) / T,
                                                   in1=g_sq[:, :], op0=ALU.mult, op1=ALU.add).then_inc(gn_step.sem, 1)

                def group_variance(b, layer=layer):
                    dve.wait_ge(gn_var_acc.sem, gn_var_acc.at(layer, b, 1))
                    nc.vector.tensor_reduce(g_sum[:, :], gen_ps[:, 0:CT * PARTS].rearrange("p (c g) -> p c g", g=PARTS),
                                            AX_X, ALU.add).then_inc(gn_step.sem, 1)
                    dve.wait_ge(gn_step.sem, gn_step.at(layer, b, 5))
                    nc.vector.tensor_scalar(g_var[:, :], g_sum[:, :], EPS, None, ALU.add).then_inc(gn_step.sem, 1)

                def normalise(b, ct, layer=layer):
                    dve.wait_ge(x_loaded[ct % 2].sem, x_loaded[ct % 2].at(layer, b, 2 + ct // 2 + 1))
                    dve.wait_ge(gn_coef.sem, gn_coef.at(layer, b, 4))
                    nc.vector.tensor_scalar(x_in[:, ct % 2, :], x_in[:, ct % 2, :], g_scale[:, ct:ct + 1],
                                            g_shift[:, ct:ct + 1], ALU.mult, ALU.add).then_inc(x_norm.sem, 1)
                    dve.wait_ge(x_high.sem, x_high.at(layer, b, ct + 1))
                    nc.vector.tensor_tensor(xn[:, 1, ct, :], x_in[:, ct % 2, :], xn[:, 0, ct, :].bitcast(F32),
                                            ALU.subtract).then_inc(x_low.sem, 1)

                def split_k(b, pair, half):
                    n, ring, cs = 2 * pair + half, pair % 2, columns_of(half, HALF)
                    dve.wait_ge(k_high.sem, k_high.at(layer, b, n + 1))
                    for head in range(2):
                        own, other = OWN[head], OTHER[head]
                        op = nc.vector.scalar_tensor_tensor(
                            out=k_parts[other, ring, head, cs], in0=gen_ps[own, :], scalar=bk[own, pair:pair + 1],
                            in1=k_parts[own, ring, head, cs].bitcast(F32), op0=ALU.add, op1=ALU.subtract)
                    op.then_inc(k_low_done.sem, 1)

                def split_q(b, u):
                    ring, pair = u % 2, u // 2
                    dve.wait_ge(q_high.sem, q_high.at(layer, b, u + 1))
                    for head in range(2):
                        own = OWN[head]
                        op = nc.vector.scalar_tensor_tensor(
                            out=q_low[own, ring, head, :], in0=gen_ps[own, :], scalar=bqs[own, pair:pair + 1],
                            in1=q_both[own, ring, head, :].bitcast(F32), op0=ALU.add, op1=ALU.subtract)
                    op.then_inc(q_low_done.sem, 1)

                def take_v(b, jt):
                    dve.wait_ge(v_acc.sem, v_acc.at(layer, b, jt + 1))
                    dve.wait_ge(pv_acc.sem, pv_acc.at(layer, b, 0))
                    src = gen_ps if jt % 2 == 0 else acc_ps
                    nc.vector.tensor_tensor(v[:, jt, :], src[:, :], bias_rows[:, 0, :], ALU.add).then_inc(v_done.sem, 1)

                def row_max(b, u, m):
                    it, head = m // 2, m % 2
                    dve.wait_ge(max_acc.sem, max_acc.at(layer, b, 8 * u + m + 1))
                    if m == 0:
                        dve.wait_ge(mt_acc.sem, mt_acc.at(layer, b, u))
                    col = MAX_ROWS[head][0]
                    nc.vector.tensor_reduce(neg_max[:, it, col:col + 1], max_ps[:, :, :].rearrange("p a n -> p (a n)"),
                                            AX_X, ALU.max, negate=True).then_inc(max_done.sem, 1)

                def split_max(b, u):
                    dve.wait_ge(m_high.sem, m_high.at(layer, b, u + 1))
                    for head in range(2):
                        hi, lo = MAX_ROWS[head]
                        op = nc.vector.tensor_tensor(q_low[lo:lo + 1, u % 2, head, :], gen_ps[hi:hi + 1, :],
                                                     q_low[hi:hi + 1, u % 2, head, :].bitcast(F32), ALU.subtract)
                    op.then_inc(m_low.sem, 1)

                def scale_context(b, u):
                    dve.wait_ge(l_acc.sem, l_acc.at(layer, b, u + 1))
                    dve.wait_ge(ctx_done.sem, ctx_done.at(layer, b, u))
                    nc.vector.reciprocal(inv_sum[:, :], gen_ps[:, :]).then_inc(inv_done.sem, 1)
                    dve.wait_ge(inv_done.sem, inv_done.at(layer, b, u + 1))
                    dve.wait_ge(ctx_raw.sem, ctx_raw.at(layer, b, u + 1))
                    part = heads_out[:, u // 2, columns_of(u % 2, HALF)]
                    nc.vector.tensor_tensor(part, part, inv_sum[:, :], ALU.mult).then_inc(ctx_done.sem, 1)

                def out_token(b, n):
                    r = n % 2
                    dve.wait_ge(o_acc.sem, o_acc.at(layer, b, n + 1))
                    dve.wait_ge(zt_acc.sem, zt_acc.at(layer, b, max(n - 1, 0)))
                    nc.vector.tensor_tensor(y_tok[:, r, :], max_ps[:, r, :], bias_rows[:, 1, :], ALU.add)\
                        .then_inc(y_done.sem, 1)
                    dve.wait_ge(y_done.sem, y_done.at(layer, b, n + 1))
                    nc.vector.bn_stats(ln_bn[:, r, :], y_tok[:, r, :]).then_inc(ln_stat.sem, 1)
                    dve.wait_ge(ln_stat.sem, ln_stat.at(layer, b, 4 * n + 1))
                    halves = ln_bn[:, r, :].rearrange("p (g k) -> p k g", k=3)
                    nc.vector.tensor_reduce(ln_sums[:, r, :], halves[:, 1:3, :], AX_X, ALU.add)
                    nc.vector.tensor_tensor(ln_diff[:, r, :], ln_bn[:, r, 1:2], ln_bn[:, r, 4:5], ALU.subtract)\
                        .then_inc(ln_stat.sem, 1)
                    dve.wait_ge(ln_stat.sem, ln_stat.at(layer, b, 4 * n + 2))
                    nc.vector.tensor_scalar(ln_mean[:, r, :], ln_sums[:, r, 0:1], 0.5, None, ALU.mult)
                    nc.vector.tensor_scalar(ln_within[:, r, :], ln_sums[:, r, 1:2], 1.0 / C, EPS, ALU.mult, ALU.add)
                    nc.vector.scalar_tensor_tensor(out=ln_between[:, r, :], in0=ln_diff[:, r, :], scalar=0.25,
                                                   in1=ln_diff[:, r, :], op0=ALU.mult, op1=ALU.mult)\
                        .then_inc(ln_stat.sem, 1)
                    dve.wait_ge(ln_stat.sem, ln_stat.at(layer, b, 4 * n + 3))
                    dve.wait_ge(ln_pow.sem, ln_pow.at(layer, b, max(n - 1, 0)))
                    nc.vector.tensor_tensor(ln_var[:, r, :], ln_within[:, r, :], ln_between[:, r, :], ALU.add)\
                        .then_inc(ln_stat.sem, 1)

                def norm_token(b, n):
                    r = n % 2
                    dve.wait_ge(ln_pow.sem, ln_pow.at(layer, b, n + 1))
                    nc.vector.tensor_scalar(y_tok[:, r, :], y_tok[:, r, :], ln_mean[:, r, :], ln_rstd[:, r, :],
                                            ALU.subtract, ALU.mult).then_inc(z_done.sem, 1)

                def add_residual(b, n):
                    r = n % 2
                    dve.wait_ge(res_in[r].sem, res_in[r].at(layer, b, n // 2 + 1))
                    if layer == 0:
                        dve.wait_ge(ln_done.sem, ln_done.at(layer, b, n + 1))
                        nc.vector.tensor_tensor(y_out[:, r, :], y_out[:, r, :], x_res[:, r, :], ALU.add)\
                            .then_inc(out_done.sem, 1)
                    else:
                        dve.wait_ge(o_acc.sem, o_acc.at(layer, b, n + 1))
                        dve.wait_ge(stored[r].sem, stored[r].at(layer, b, n // 2))
                        nc.vector.scalar_tensor_tensor(out=y_out[:, r, :], in0=max_ps[:, r, :],
                                                       scalar=cols[:, 4, n % CT:n % CT + 1], in1=x_res[:, r, :],
                                                       op0=ALU.add, op1=ALU.add).then_inc(out_done.sem, 1)

                def out_step(b, n):
                    if layer == 1:
                        if n < OUT_TILES:
                            add_residual(b, n)
                        return
                    if n < OUT_TILES:
                        out_token(b, n)
                    if 1 <= n <= OUT_TILES:
                        norm_token(b, n - 1)
                    if n >= 2:
                        add_residual(b, n - 2)

                dve.wait_ge(layer_in, 64 * (layer + 1))
                if layer:
                    dve.wait_ge(q_low_done.sem, q_low_done.at(layer, 0, 0))
                nc.vector.tensor_scalar(bqs[:, :], bq, QUERY_SCALE[layer], None, ALU.mult).then_inc(prep_done, 1)
                dve.wait_ge(prep_done, 2 * layer + 1)
                for ct in range(CT):
                    image_stats(0, ct)
                group_deviation(0)
                split_w(0, 0)
                split_w(0, 1)
                group_variance(0)
                for ct in range(CT):
                    normalise(0, ct)
                dve.wait_ge(wv_high, layer + 1)
                nc.vector.tensor_tensor(wv[:, 1, :, :], v[:, 0:CT, :], wv[:, 0, :, :].bitcast(F32), ALU.subtract)\
                    .then_inc(prep_done, 1)
                dve.wait_ge(prep_done, 2 * layer + 2)

                with dve.Fori(0, B) as b:
                    split_k(b, 0, 0)
                    split_k(b, 0, 1)
                    split_q(b, 0)
                    for jt in range(KT):
                        take_v(b, jt)
                        row_max(b, 0, jt)
                    split_max(b, 0)
                    for u in range(UNITS):
                        pair, half = u // 2, u % 2
                        for s in range(STEPS):
                            if u + 1 < UNITS:
                                if half == 1 and s < 2:
                                    split_k(b, pair + 1, s)
                                if s == (2 if half else 0):
                                    split_q(b, u + 1)
                            if s == 3 and u > 0:
                                scale_context(b, u - 1)
                            if u + 1 < UNITS and 3 <= s < 7:
                                row_max(b, u + 1, 2 * (s - 3))
                                row_max(b, u + 1, 2 * (s - 3) + 1)
                            if s == 6 and u in (1, 3, 5):
                                split_w(b, 2 + u // 2)
                            if u in (2, 4) and s in (1, 2):
                                image_stats(b + 1, u - 2 + s - 1)
                            if (u, s) == (4, 4):
                                group_deviation(b + 1)
                            if (u, s) == (5, 5):
                                group_variance(b + 1)
                            if u == UNITS - 1:
                                if s < CT:
                                    normalise(b + 1, s)
                                if s == 4:
                                    split_w(b, 5)
                                if s >= 5:
                                    out_step(b, s - 5)
                        if u + 1 < UNITS:
                            split_max(b, u + 1)
                    out_step(b, 3)
                    scale_context(b, UNITS - 1)
                    for n in range(4, OUT_TILES + 2):
                        out_step(b, n)

        @block.gpsimd
        def _(pool):
            for counter in counts:
                pool.sem_inc(counter.sem, 1)
            nc.gpsimd.memset(k_ones[:, :, :, :].bitcast(F32), 0.0).then_inc(zeroed, 1)
            nc.gpsimd.memset(q_low[:, :, :, :].bitcast(F32), 0.0).then_inc(zeroed, 1)
            nc.gpsimd.memset(minus_half[:, :], -0.5)
            nc.gpsimd.memset(neg_max[:, :, :], 0.0).then_inc(zeroed, 1)
            pool.wait_ge(zeroed, 3)
            for head in range(2):
                for row in MAX_ROWS[head]:
                    op = nc.gpsimd.memset(k_ones[row:row + 1, :, head, :].bitcast(F32), 1.0)
            op.then_inc(zeroed, 1)
            pool.wait_ge(zeroed, 4)
            for layer in range(LAYERS):
                def coefficients(b, layer=layer):
                    step = lambda k: pool.wait_ge(gn_coef.sem, gn_coef.at(layer, b, k))
                    pool.wait_ge(gn_step.sem, gn_step.at(layer, b, 6))
                    pool.wait_ge(x_norm.sem, x_norm.at(layer, b, 0))
                    nc.gpsimd.tensor_tensor(g_rstd[:, :], g_var[:, :], minus_half[:, :], ALU.pow).then_inc(gn_coef.sem, 1)
                    step(1)
                    nc.gpsimd.tensor_tensor(g_scale[:, :], g_rstd[:, :], gamma, ALU.mult).then_inc(gn_coef.sem, 1)
                    step(2)
                    nc.gpsimd.tensor_tensor(g_tmp[:, :], g_mean[:, :], g_scale[:, :], ALU.mult).then_inc(gn_coef.sem, 1)
                    step(3)
                    nc.gpsimd.tensor_tensor(g_shift[:, :], beta, g_tmp[:, :], ALU.subtract).then_inc(gn_coef.sem, 1)

                def sum_step(b, u, s):
                    head, n = s % 2, STEPS * u + s
                    part = [e[:, s % RING, i, :] for i in range(2)]
                    total = e_sum[:, head, :]
                    pool.wait_ge(exp_done.sem, exp_done.at(layer, b, n + 1))
                    if s < 2:
                        pool.wait_ge(l_acc.sem, l_acc.at(layer, b, u))
                        nc.gpsimd.tensor_tensor(total, part[0], part[1], ALU.add).then_inc(sum_done.sem, 1)
                        return
                    pool.wait_ge(sum_done.sem, sum_done.at(layer, b, n - 1))
                    nc.gpsimd.tensor_tensor(total, total, part[0], ALU.add).then_inc(sum_part.sem, 1)
                    pool.wait_ge(sum_part.sem, sum_part.at(layer, b, 6 * u + s - 1))
                    nc.gpsimd.tensor_tensor(total, total, part[1], ALU.add).then_inc(sum_done.sem, 1)

                def out_step(b, n):
                    if layer == 0 and n < OUT_TILES:
                        r = n % 2
                        pool.wait_ge(ln_stat.sem, ln_stat.at(layer, b, 4 * n + 4))
                        pool.wait_ge(z_done.sem, z_done.at(layer, b, max(n - 1, 0)))
                        nc.gpsimd.tensor_tensor(ln_rstd[:, r, :], ln_var[:, r, :], minus_half[:, 0:1], ALU.pow)\
                            .then_inc(ln_pow.sem, 1)

                pool.wait_ge(layer_in, 64 * (layer + 1))
                coefficients(0)
                with pool.Fori(0, B) as b:
                    for u in range(UNITS):
                        for s in range(STEPS):
                            sum_step(b, u, s)
                            if (u, s) == (5, 6):
                                coefficients(b + 1)
                            if u == UNITS - 1 and s >= 5:
                                out_step(b, s - 5)
                    for n in range(3, OUT_TILES):
                        out_step(b, n)


def kernel(**inputs):
    import numpy as np
    import concourse.bacc as bacc
    from concourse.bass_utils import run_bass_kernel_spmd

    def by_channel(vector):
        return vector.reshape(CT, P).T

    def transposed(w):
        return np.ascontiguousarray(w.T.reshape(CT, P, C).transpose(1, 0, 2))

    def by_pair(w):
        return w.reshape(PAIRS, P, CT, P).transpose(0, 3, 2, 1).reshape(PAIRS, P, CT * P)

    a = {name: np.asarray(value) for name, value in inputs.items()}
    x = a["x"].reshape(B, C, T)
    qkv_w, qkv_b = a["L1_conv_qkv_w"], a["L1_conv_qkv_b"]
    wq = [a["L0_conv_wq"], qkv_w[0:C]]
    wk = [a["L0_conv_wk"], qkv_w[C:2 * C]]
    wv = [a["L0_conv_wv"], qkv_w[2 * C:3 * C]]
    wo = [a["L0_conv_wo"], a["L1_conv_proj_w"]]
    per_channel = [
        [a["L0_conv_gn_gamma"], a["L0_conv_gn_beta"], a["L0_conv_bq"], a["L0_conv_bk"],
         a["L0_conv_ln_gamma"], a["L0_conv_ln_beta"]],
        [a["L1_conv_gn_scale"], a["L1_conv_gn_bias"], qkv_b[0:C], qkv_b[C:2 * C],
         a["L1_conv_proj_b"], a["L1_conv_proj_b"]],
    ]
    per_row = [[a["L0_conv_bv"], a["L0_conv_bo"]], [qkv_b[2 * C:3 * C], a["L1_conv_proj_b"]]]
    group = C // GROUPS
    constants = np.concatenate([
        np.eye(P, dtype=np.float32),
        np.kron(np.eye(P // group, dtype=np.float32), np.full((group, group), 1.0 / (group * PARTS), np.float32)),
        np.ones((P, D), np.float32),
    ], axis=1)

    arrays = {"in_x": x, "in_constants": constants}
    for layer in range(LAYERS):
        arrays[f"in_wqk{layer}"] = np.stack([by_pair(wq[layer]), by_pair(wk[layer])], axis=1)
        arrays[f"in_wv{layer}"] = transposed(wv[layer])
        arrays[f"in_wo{layer}"] = transposed(wo[layer])
        arrays[f"in_columns{layer}"] = np.stack([by_channel(c) for c in per_channel[layer]], axis=1)
        arrays[f"in_rows{layer}"] = np.stack(per_row[layer])
    arrays = {name: np.ascontiguousarray(value) for name, value in arrays.items()}

    nc = bacc.Bacc("TRN2", target_bir_lowering=False, num_devices=1)
    dram = {name: nc.dram_tensor(name, value.shape, F32, kind="ExternalInput").ap() for name, value in arrays.items()}
    middle = nc.dram_tensor("middle", [B, C, T], F32).ap()
    out = nc.dram_tensor("out", [B, C, T], F32, kind="ExternalOutput").ap()
    attention_blocks(nc, dram["in_x"], out, middle, [dram[f"in_wqk{i}"] for i in range(LAYERS)],
                     [dram[f"in_wv{i}"] for i in range(LAYERS)], [dram[f"in_wo{i}"] for i in range(LAYERS)],
                     [dram[f"in_columns{i}"] for i in range(LAYERS)], [dram[f"in_rows{i}"] for i in range(LAYERS)],
                     dram["in_constants"])
    result = run_bass_kernel_spmd(nc, [arrays], core_ids=[0])
    return result.results[0]["out"].reshape(B, C, 32, 32)
```

```python
from contextlib import ExitStack

import concourse.bass as bass
from concourse import mybir

F32 = mybir.dt.float32
F32R = mybir.dt.float32r
ALU = mybir.AluOpType
ACT = mybir.ActivationFunctionType
AX_X = mybir.AxisListType.X

P = 128
B, C, T = 8, 512, 1024
HEADS, D = 8, 64
GROUPS = 32
EPS = 1e-5
CT = C // P
PAIRS = HEADS // 2
HALF = T // 2
UNITS = 2 * PAIRS
KT = T // P
STEPS = 2 * KT
RING = 8
ADDS = 2 * (KT - 1)
MAX_STEPS = 2 * HALF // P
MAX_AFTER = (4, 5, 7, 8, 10, 11, 12, 13)
SUM_AFTER = 7
FIRST_BEFORE = (5, 7, 8)
QUERY_TILES = HALF // P
OUT_TILES = 8
LAYERS = 2
PARTS = 4
QUERY_SCALE = (float(D) ** -0.25, float(D) ** -0.5)


class Count:

    def __init__(self, sem, per_image, ahead=0, by=1):
        self.sem, self.per_image, self.ahead, self.by = sem, per_image, ahead, by

    def at(self, layer, b, k):
        return (layer * (B * self.per_image + self.ahead) + k) * self.by + 1 + b * (self.per_image * self.by)


def attention_blocks(nc, x, out, middle, weights, wv_in, wo_in, columns, rows, constants):
    with ExitStack() as ctx_:
        def sb(name, shape, dt=F32):
            return ctx_.enter_context(nc.sbuf_tensor(name, shape, dt))

        def psum(name, shape):
            return ctx_.enter_context(nc.psum_tensor(name, shape, F32))

        def sem(name):
            return ctx_.enter_context(nc.semaphore(name))

        counts = []

        def count(name, per_image, ahead=0, by=1):
            counts.append(Count(sem(name), per_image, ahead, by))
            return counts[-1]

        consts = sb("consts", [P, 2 * P + D])
        identity, group_mean, ones = consts[:, 0:P], consts[:, P:2 * P], consts[:, 2 * P:2 * P + D]
        cols = sb("cols", [P, 6, CT])
        gamma, beta, bq, bk = (cols[:, i, :] for i in range(4))
        bias_rows = sb("bias_rows", [P, 2, C])
        bqs = sb("bqs", [P, CT])
        wv = sb("wv", [P, 2, CT, C], F32R)
        wo = sb("wo", [P, CT, C])
        wqk_raw = sb("wqk_raw", [P, CT * P])
        wqk = sb("wqk", [P, 2, 2, 2, CT * P], F32R)
        x_in = sb("x_in", [P, 2, T])
        xn = sb("xn", [P, 2, CT, T], F32R)
        q_both = sb("q_both", [P, 2, 2, HALF], F32R)
        q_low = sb("q_low", [P, 2, 2, HALF], F32R)
        k_sets = sb("k_sets", [P, 2, 2, 2, T], F32R)
        k_parts, k_ones = k_sets[:, 0], k_sets[:, 1]
        v = sb("v", [P, KT, C])
        e = sb("e", [P, RING, HALF])
        e_sum = sb("e_sum", [P, 2, 2, HALF])
        inv_sum = sb("inv_sum", [P, 2, P])
        neg_max = sb("neg_max", [P, QUERY_TILES, D + 1])
        heads_out = sb("heads_out", [P, CT, T])
        x_res = sb("x_res", [P, 2, HALF])
        y_out = sb("y_out", [P, 2, HALF])
        y_tok = sb("y_tok", [P, 2, C])
        bn = sb("bn", [P, CT, 3 * PARTS])
        part_means, part_squares = (bn[:, :, :].rearrange("p c (g k) -> p (c g) k", k=3)[:, :, i] for i in (1, 2))
        g_mean = sb("g_mean", [P, CT])
        g_dev = sb("g_dev", [P, CT * PARTS])
        g_sq = sb("g_sq", [P, CT * PARTS])
        g_exp = sb("g_exp", [P, CT * PARTS])
        g_sum = sb("g_sum", [P, CT])
        g_var = sb("g_var", [P, CT])
        g_rstd = sb("g_rstd", [P, CT])
        g_scale = sb("g_scale", [P, CT])
        g_tmp = sb("g_tmp", [P, CT])
        g_shift = sb("g_shift", [P, CT])
        minus_half = sb("minus_half", [P, CT])
        ln_bn = sb("ln_bn", [P, 2, 6])
        ln_sums = sb("ln_sums", [P, 2, 2])
        ln_diff = sb("ln_diff", [P, 2, 1])
        ln_mean = sb("ln_mean", [P, 2, 1])
        ln_within = sb("ln_within", [P, 2, 1])
        ln_between = sb("ln_between", [P, 2, 1])
        ln_var = sb("ln_var", [P, 2, 1])
        ln_rstd = sb("ln_rstd", [P, 2, 1])

        scores_ps = psum("scores_ps", [P, 2, HALF])
        max_ps = psum("max_ps", [P, 2, HALF])
        acc_ps = psum("acc_ps", [P, HALF])
        q_ps = psum("q_ps", [P, HALF])
        k_ps = psum("k_ps", [P, HALF])
        gen_ps = psum("gen_ps", [P, HALF])

        k_acc = count("k_acc", 2 * PAIRS, 2)
        q_acc = count("q_acc", UNITS, 1)
        v_acc = count("v_acc", KT)
        max_acc = count("max_acc", MAX_STEPS * UNITS)
        mt_acc = count("mt_acc", UNITS)
        s_acc = count("s_acc", STEPS * UNITS)
        pv_acc = count("pv_acc", KT * UNITS)
        l_acc = count("l_acc", UNITS)
        o_acc = count("o_acc", OUT_TILES)
        gn_mean_acc = count("gn_mean_acc", 1, 1)
        gn_var_acc = count("gn_var_acc", 1, 1)
        zt_acc = count("zt_acc", OUT_TILES)
        w_high = count("w_high", 2 * PAIRS, 4)
        k_high = count("k_high", 4 * PAIRS, 4)
        q_high = count("q_high", 2 * UNITS, 2)
        m_high = count("m_high", 2 * UNITS)
        exp_done = count("exp_done", STEPS * UNITS)
        x_high = count("x_high", CT, CT)
        ctx_raw = count("ctx_raw", UNITS)
        ln_done = count("ln_done", OUT_TILES)
        wv_high = sem("wv_high")
        w_low = count("w_low", 2 * PAIRS, 4)
        k_low_done = count("k_low_done", 4 * PAIRS, 4)
        q_low_done = count("q_low_done", 2 * UNITS, 2)
        m_low = count("m_low", 2 * UNITS)
        max_done = count("max_done", MAX_STEPS * UNITS)
        v_done = count("v_done", KT)
        inv_done = count("inv_done", QUERY_TILES * UNITS)
        ctx_done = count("ctx_done", QUERY_TILES * UNITS)
        bn_done = count("bn_done", CT, CT)
        gn_step = count("gn_step", 6, 6)
        x_norm = count("x_norm", CT, CT)
        x_low = count("x_low", CT, CT)
        y_done = count("y_done", OUT_TILES)
        ln_stat = count("ln_stat", 4 * OUT_TILES)
        z_done = count("z_done", OUT_TILES)
        out_done = count("out_done", OUT_TILES)
        prep_done = sem("prep_done")
        zeroed = sem("zeroed")
        sum_done = count("sum_done", ADDS * UNITS)
        gn_coef = count("gn_coef", 4, 4)
        ln_pow = count("ln_pow", OUT_TILES)
        setup_in = sem("setup_in")
        layer_in = sem("layer_in")
        wv_in_sem = sem("wv_in_sem")
        w_in = count("w_in", 2 * PAIRS, 4, by=16)
        x_loaded = [count(f"x_loaded{i}", CT, CT, by=16) for i in range(2)]
        res_in = [count(f"res_in{i}", OUT_TILES // 2, by=16) for i in range(2)]
        stored = [count(f"stored{i}", OUT_TILES // 2, by=16) for i in range(2)]

        block = ctx_.enter_context(nc.Block())
        LOW, TOP = slice(0, D), slice(D, P)
        OWN = (LOW, TOP)
        OTHER = (TOP, LOW)
        MAX_ROWS = ((D, D + 32), (0, 32))

        def columns_of(tile, n=P):
            return slice(tile * n, (tile + 1) * n)

        @block.sync
        def _(sp):
            sp.dma_start(consts[:], constants).then_inc(setup_in, 16)
            for layer in range(LAYERS):
                source = x if layer == 0 else middle
                target = middle if layer == 0 else out

                def load_stats(gi_b, img, ct, layer=layer, source=source):
                    if ct < 2:
                        sp.wait_ge(x_low.sem, x_low.at(layer, gi_b, 0))
                    else:
                        sp.wait_ge(bn_done.sem, bn_done.at(layer, gi_b, ct - 1))
                    sp.dma_start(x_in[:, ct % 2, :], source[img, columns_of(ct), :])\
                        .then_inc(x_loaded[ct % 2].sem, 16)

                def load_norm(gi_b, img, ct, layer=layer, source=source):
                    if ct < 2:
                        sp.wait_ge(bn_done.sem, bn_done.at(layer, gi_b, ct + 3))
                    else:
                        sp.wait_ge(x_low.sem, x_low.at(layer, gi_b, ct - 1))
                    sp.dma_start(x_in[:, ct % 2, :], source[img, columns_of(ct), :])\
                        .then_inc(x_loaded[ct % 2].sem, 16)

                def load_w(b, k, which, layer=layer):
                    sp.wait_ge(w_high.sem, w_high.at(layer, b, 2 * k + which))
                    sp.wait_ge(w_low.sem, w_low.at(layer, b, 2 * k + which))
                    sp.dma_start(wqk_raw[:, :], weights[layer][k % PAIRS, which]).then_inc(w_in.sem, 16)

                if layer:
                    for ring in range(2):
                        sp.wait_ge(stored[ring].sem, stored[ring].at(layer, 0, 0))
                    sp.wait_ge(x_low.sem, x_low.at(layer, 0, 0))
                sp.dma_start(cols[:, :, :], columns[layer]).then_inc(layer_in, 16)
                for i in range(2):
                    sp.dma_start(bias_rows[:, i, :], rows[layer][i:i + 1, :].broadcast_to([P, C])).then_inc(layer_in, 16)
                sp.dma_start(wo[:, :, :], wo_in[layer]).then_inc(layer_in, 16)
                for ct in range(CT):
                    load_stats(0, 0, ct)
                for k in range(2):
                    for which in range(2):
                        load_w(0, k, which)
                for ct in range(CT):
                    load_norm(0, 0, ct)
                sp.dma_start(v[:, 0:CT, :], wv_in[layer]).then_inc(wv_in_sem, 16)

                with sp.Fori(0, B) as b:
                    nxt = (b + 1) % B
                    load_w(b, 2, 0)
                    load_stats(b + 1, nxt, 0)
                    load_stats(b + 1, nxt, 1)
                    load_w(b, 2, 1)
                    load_w(b, 3, 0)
                    load_stats(b + 1, nxt, 2)
                    load_stats(b + 1, nxt, 3)
                    load_w(b, 3, 1)
                    load_w(b, 4, 0)
                    load_norm(b + 1, nxt, 0)
                    load_norm(b + 1, nxt, 1)
                    load_w(b, 4, 1)
                    load_w(b, 5, 0)

                    def load_res(n):
                        sp.wait_ge(out_done.sem, out_done.at(layer, b, max(n - 1, 0)))
                        if layer == 0:
                            src = source[b].rearrange("(c p) t -> p c t", p=P)[:, :, columns_of(n)]
                            dst = x_res[:, n % 2, :].rearrange("p (c t) -> p c t", c=CT)
                        else:
                            src = source[b, columns_of(n % CT), columns_of(n // CT, HALF)]
                            dst = x_res[:, n % 2, :]
                        sp.dma_start(dst, src).then_inc(res_in[n % 2].sem, 16)

                    load_res(0)
                    load_res(1)
                    load_norm(b + 1, nxt, 2)
                    load_norm(b + 1, nxt, 3)
                    load_w(b, 5, 1)
                    for n in range(OUT_TILES):
                        sp.wait_ge(out_done.sem, out_done.at(layer, b, n + 1))
                        if layer == 0:
                            dst = target[b].rearrange("(c p) t -> p c t", p=P)[:, :, columns_of(n)]
                            src = y_out[:, n % 2, :].rearrange("p (c t) -> p c t", c=CT)
                        else:
                            dst = target[b, columns_of(n % CT), columns_of(n // CT, HALF)]
                            src = y_out[:, n % 2, :]
                        sp.dma_start(dst, src).then_inc(stored[n % 2].sem, 16)
                        if n + 2 < OUT_TILES:
                            load_res(n + 2)
            for ring in range(2):
                sp.wait_ge(stored[ring].sem, stored[ring].at(LAYERS, 0, 0))

        @block.tensor
        def _(pe):
            pe.wait_ge(setup_in, 16)
            pe.wait_ge(zeroed, 4)
            for layer in range(LAYERS):
                gen_reader = []

                def fill_gen(*readers):
                    for counter, value in gen_reader:
                        pe.wait_ge(counter.sem, value)
                    gen_reader[:] = readers

                def group_means(b, layer=layer):
                    pe.wait_ge(bn_done.sem, bn_done.at(layer, b, CT))
                    fill_gen((gn_step, gn_step.at(layer, b, 1)))
                    pe.matmul(gen_ps[:, 0:CT * PARTS], group_mean, part_means, start=True, stop=True)\
                        .then_inc(gn_mean_acc.sem, 1)

                def group_vars(b, layer=layer):
                    pe.wait_ge(gn_step.sem, gn_step.at(layer, b, 4))
                    fill_gen((gn_step, gn_step.at(layer, b, 5)))
                    pe.matmul(gen_ps[:, 0:CT * PARTS], group_mean, g_exp[:, :], start=True, stop=True)\
                        .then_inc(gn_var_acc.sem, 1)

                def project(dst, which, pair, half, b, chunks, ready):
                    for kt in chunks:
                        for n, (w_part, x_part) in enumerate(((0, 0), (0, 1), (1, 0))):
                            mm = pe.matmul(dst, wqk[:, pair % 2, which, w_part, columns_of(kt)],
                                           xn[:, x_part, kt, columns_of(half, HALF)],
                                           start=kt == 0 and n == 0, stop=kt == CT - 1 and n == 2)
                        if kt == CT - 1:
                            mm.then_inc(ready.sem, 1)

                def k_tile(b, pair, half, chunks=range(CT)):
                    if chunks[0] == 0:
                        pe.wait_ge(w_high.sem, w_high.at(layer, b, 2 * pair + 2))
                        pe.wait_ge(w_low.sem, w_low.at(layer, b, 2 * pair + 2))
                        if (pair, half) == (1, 0):
                            pe.wait_ge(v_done.sem, v_done.at(layer, b, KT))
                        pe.wait_ge(k_low_done.sem, k_low_done.at(layer, b, 4 * pair + 2 * half))
                        pe.wait_ge(k_high.sem, k_high.at(layer, b, 4 * pair + 2 * half))
                    project(k_ps[:, :], 1, pair, half, b, chunks, k_acc)

                def q_tile(b, u, chunks=range(CT)):
                    if chunks[0] == 0:
                        pe.wait_ge(w_high.sem, w_high.at(layer, b, 2 * (u // 2) + 1))
                        pe.wait_ge(w_low.sem, w_low.at(layer, b, 2 * (u // 2) + 1))
                        if u == 1:
                            pe.wait_ge(v_done.sem, v_done.at(layer, b, KT - 1))
                        pe.wait_ge(q_low_done.sem, q_low_done.at(layer, b, 2 * u))
                        pe.wait_ge(q_high.sem, q_high.at(layer, b, 2 * u))
                    project(q_ps[:, :], 0, u // 2, u % 2, b, chunks, q_acc)

                def v_tile(b, jt):
                    dst = (q_ps, k_ps)[jt % 2]
                    if jt >= 2:
                        pe.wait_ge(v_done.sem, v_done.at(layer, b, jt - 1))
                    elif jt == 0:
                        pe.wait_ge(q_high.sem, q_high.at(layer, b, 2))
                        pe.wait_ge(q_low_done.sem, q_low_done.at(layer, b, 2))
                    else:
                        pe.wait_ge(k_high.sem, k_high.at(layer, b, 4))
                        pe.wait_ge(k_low_done.sem, k_low_done.at(layer, b, 4))
                    n = 0
                    for kt in range(CT):
                        for x_part, w_part in ((0, 0), (0, 1), (1, 0)):
                            mm = pe.matmul(dst[:, :], xn[:, x_part, kt, columns_of(jt)], wv[:, w_part, kt, :],
                                           start=n == 0, stop=n == 3 * CT - 1)
                            n += 1
                    mm.then_inc(v_acc.sem, 1)

                def max_step(b, u, m):
                    it, head = m // 2, m % 2
                    if m < 2:
                        pe.wait_ge(q_high.sem, q_high.at(layer, b, 2 * u + m + 1))
                        pe.wait_ge(k_high.sem, k_high.at(layer, b, 4 * (u // 2) + 4))
                        pe.wait_ge(k_low_done.sem, k_low_done.at(layer, b, 4 * (u // 2) + 4))
                    pe.wait_ge(max_done.sem, max_done.at(layer, b, MAX_STEPS * u + m))
                    for half in range(2):
                        mm = pe.matmul(max_ps[:, half, :], q_both[:, u % 2, head, columns_of(it)],
                                       k_parts[:, u // 2 % 2, head, columns_of(half, HALF)], start=True, stop=True)
                    mm.then_inc(max_acc.sem, 1)

                def max_rows(b, u):
                    pe.wait_ge(max_done.sem, max_done.at(layer, b, MAX_STEPS * (u + 1)))
                    fill_gen((m_high, m_high.at(layer, b, 2 * u + 2)), (m_low, m_low.at(layer, b, 2 * u + 2)))
                    for it in range(QUERY_TILES):
                        mm = pe.transpose(gen_ps[0:D + 1, columns_of(it)], neg_max[:, it, :], identity)
                    mm.then_inc(mt_acc.sem, 1)

                def score_step(b, u, h):
                    head, ring, keys = h % 2, u % 2, columns_of(h // 2)
                    if h < 2:
                        pe.wait_ge(m_high.sem, m_high.at(layer, b, 2 * u + h + 1))
                        pe.wait_ge(m_low.sem, m_low.at(layer, b, 2 * u + h + 1))
                        pe.wait_ge(q_low_done.sem, q_low_done.at(layer, b, 2 * u + h + 1))
                    pe.wait_ge(exp_done.sem, exp_done.at(layer, b, max(STEPS * u + h - 1, 0)))
                    pe.matmul(scores_ps[:, h % 2, :], k_parts[:, u // 2 % 2, head, keys],
                              q_both[:, ring, head, :], start=True, stop=False)
                    pe.matmul(scores_ps[:, h % 2, :], k_ones[:, u // 2 % 2, head, keys],
                              q_low[:, ring, head, :], start=False, stop=True).then_inc(s_acc.sem, 1)

                def value_step(b, u, jt):
                    pe.wait_ge(exp_done.sem, exp_done.at(layer, b, STEPS * u + 2 * jt + 2))
                    if jt == 0:
                        if u == 0:
                            pe.wait_ge(v_done.sem, v_done.at(layer, b, KT))
                        pe.wait_ge(ctx_raw.sem, ctx_raw.at(layer, b, u))
                    for head in range(2):
                        at = (2 * (u // 2) + head) * D
                        mm = pe.matmul(acc_ps[OWN[head], :], v[:, jt, at:at + D],
                                       e[:, (2 * jt + head) % RING, :], start=jt == 0, stop=jt == KT - 1)
                    mm.then_inc(pv_acc.sem, 1)

                def sum_step(b, u):
                    pe.wait_ge(sum_done.sem, sum_done.at(layer, b, ADDS * (u + 1)))
                    fill_gen((inv_done, inv_done.at(layer, b, QUERY_TILES * (u + 1))))
                    for head in range(2):
                        mm = pe.matmul(gen_ps[OWN[head], :], ones, e_sum[:, u % 2, head, :], start=True, stop=True)
                    mm.then_inc(l_acc.sem, 1)

                def out_tile(b, n):
                    pe.wait_ge(ctx_done.sem, ctx_done.at(layer, b, QUERY_TILES * (UNITS - 1 + n // 4)))
                    if n < 2:
                        pe.wait_ge(max_done.sem, max_done.at(layer, b, MAX_STEPS * UNITS))
                    else:
                        reader = y_done if layer == 0 else out_done
                        pe.wait_ge(reader.sem, reader.at(layer, b, n - 1))
                    for kt in range(CT):
                        if layer == 0:
                            lhs, rhs = heads_out[:, kt, columns_of(n)], wo[:, kt, :]
                        else:
                            lhs, rhs = wo[:, kt, columns_of(n % CT)], heads_out[:, kt, columns_of(n // CT, HALF)]
                        mm = pe.matmul(max_ps[:, n % 2, :], lhs, rhs, start=kt == 0, stop=kt == CT - 1)
                    mm.then_inc(o_acc.sem, 1)

                def token_turn(b, n):
                    pe.wait_ge(z_done.sem, z_done.at(layer, b, n + 1))
                    fill_gen((ln_done, ln_done.at(layer, b, n + 1)))
                    for ct in range(CT):
                        mm = pe.transpose(gen_ps[:, columns_of(ct)], y_tok[:, n % 2, columns_of(ct)], identity)
                    mm.then_inc(zt_acc.sem, 1)

                def out_step(b, n):
                    if n < OUT_TILES:
                        out_tile(b, n)
                    if layer == 0 and n >= 2:
                        token_turn(b, n - 2)

                if layer:
                    gen_reader[:] = [(ln_done, ln_done.at(1, 0, 0)), (inv_done, inv_done.at(1, 0, 0))]
                group_means(0)
                group_vars(0)
                pe.wait_ge(layer_in, 64 * (layer + 1))
                pe.wait_ge(prep_done, 2 * (layer + 1))
                pe.wait_ge(wv_high, layer + 1)

                def first_of(b, which):
                    if which == 0:
                        pe.wait_ge(x_high.sem, x_high.at(layer, b, CT))
                        pe.wait_ge(x_low.sem, x_low.at(layer, b, CT))
                        k_tile(b, 0, 0)
                    elif which == 1:
                        q_tile(b, 0)
                    else:
                        k_tile(b, 0, 1)

                for which in range(3):
                    first_of(0, which)

                with pe.Fori(0, B) as b:
                    gen_reader[:] = [(gn_step, gn_step.at(layer, b, 6)),
                                     (inv_done, inv_done.at(layer, b, 0))]
                    if layer == 0:
                        gen_reader.append((ln_done, ln_done.at(layer, b, 0)))
                    last_out = y_done if layer == 0 else out_done
                    for jt in range(KT):
                        v_tile(b, jt)
                        if jt == 0:
                            pe.wait_ge(last_out.sem, last_out.at(layer, b, 0))
                        max_step(b, 0, jt)
                    max_rows(b, 0)
                    for u in range(UNITS):
                        last = u == UNITS - 1
                        for h in range(STEPS):
                            score_step(b, u, h)
                            if h >= 4 and h % 2 == 0:
                                value_step(b, u, h // 2 - 2)
                            if not last:
                                if h < 2:
                                    q_tile(b, u + 1, (2 * h, 2 * h + 1))
                                if h in MAX_AFTER:
                                    max_step(b, u + 1, MAX_AFTER.index(h))
                                if u % 2 == 0 and u // 2 + 1 < PAIRS:
                                    if 2 <= h < 6:
                                        k_tile(b, u // 2 + 1, 0, (h - 2,))
                                    if 8 <= h < 12:
                                        k_tile(b, u // 2 + 1, 1, (h - 8,))
                            if h == SUM_AFTER and u > 0:
                                sum_step(b, u - 1)
                            if (u, h) == (4, 12):
                                group_means(b + 1)
                            if (u, h) == (5, 12):
                                group_vars(b + 1)
                        if not last:
                            max_rows(b, u + 1)
                        value_step(b, u, KT - 2)
                        value_step(b, u, KT - 1)
                    for n in range(OUT_TILES + 2):
                        if n == 2:
                            sum_step(b, UNITS - 1)
                        if n in FIRST_BEFORE:
                            first_of(b + 1, FIRST_BEFORE.index(n))
                        out_step(b, n)

        @block.scalar
        def _(act):
            act.wait_ge(zeroed, 4)
            for layer in range(LAYERS):
                def split_w(b, k, which, layer=layer):
                    act.wait_ge(w_in.sem, w_in.at(layer, b, 2 * k + which + 1))
                    act.wait_ge(q_acc.sem, q_acc.at(layer, b, max(2 * (k - 1), 0)))
                    nc.scalar.activation(wqk[:, k % 2, which, 0, :], wqk_raw[:, :], ACT.Copy,
                                         scale=1.0 if which else QUERY_SCALE[layer]).then_inc(w_high.sem, 1)

                def split_x(b, ct, layer=layer):
                    act.wait_ge(x_norm.sem, x_norm.at(layer, b, ct + 1))
                    nc.scalar.activation(xn[:, 0, ct, :], x_in[:, ct % 2, :], ACT.Copy).then_inc(x_high.sem, 1)

                def split_k(b, pair, half, head):
                    own, ring = OWN[head], pair % 2
                    act.wait_ge(k_acc.sem, k_acc.at(layer, b, 2 * pair + half + 1))
                    act.wait_ge(s_acc.sem, s_acc.at(layer, b, max(2 * STEPS * (pair - 1), 0)))
                    both = k_ps[own, :].rearrange("p (a n) -> p a n", a=1).broadcast_to([D, 2, HALF])
                    nc.scalar.activation(k_sets[own, :, ring, head, columns_of(half, HALF)], both,
                                         ACT.Identity, bias=bk[own, pair % PAIRS:pair % PAIRS + 1]).then_inc(k_high.sem, 1)

                def split_q(b, u, head):
                    own, ring, pair = OWN[head], u % 2, u // 2 % PAIRS
                    act.wait_ge(q_acc.sem, q_acc.at(layer, b, u + 1))
                    act.wait_ge(s_acc.sem, s_acc.at(layer, b, max(STEPS * (u - 1), 0)))
                    for place in (own, OTHER[head]):
                        op = nc.scalar.activation(q_both[place, ring, head, :], q_ps[own, :],
                                                  ACT.Identity, bias=bqs[own, pair:pair + 1])
                    op.then_inc(q_high.sem, 1)

                def split_max(b, u):
                    act.wait_ge(mt_acc.sem, mt_acc.at(layer, b, u + 1))
                    act.wait_ge(s_acc.sem, s_acc.at(layer, b, max(STEPS * (u - 1), 0)))
                    for head in range(2):
                        row = MAX_ROWS[head][0]
                        nc.scalar.activation(q_low[row:row + 1, u % 2, head, :], gen_ps[row:row + 1, :], ACT.Copy)\
                            .then_inc(m_high.sem, 1)

                def exp_step(b, u, h):
                    act.wait_ge(s_acc.sem, s_acc.at(layer, b, STEPS * u + h + 1))
                    old_u, old_h = divmod(STEPS * u + h - RING, STEPS)
                    used = KT * old_u + old_h // 2 + 1 if old_u >= 0 else 0
                    added = ADDS * old_u + 2 * max(old_h // 2 - 1, 0) + old_h % 2 + 1 if old_u >= 0 else 0
                    act.wait_ge(pv_acc.sem, pv_acc.at(layer, b, used))
                    act.wait_ge(sum_done.sem, sum_done.at(layer, b, added))
                    nc.scalar.activation(e[:, h % RING, :], scores_ps[:, h % 2, :], ACT.Exp).then_inc(exp_done.sem, 1)

                def take_context(b, u):
                    act.wait_ge(pv_acc.sem, pv_acc.at(layer, b, KT * (u + 1)))
                    if u < 2:
                        act.wait_ge(o_acc.sem, o_acc.at(layer, b, 0))
                    nc.scalar.activation(heads_out[:, u // 2, columns_of(u % 2, HALF)], acc_ps[:, :], ACT.Copy)\
                        .then_inc(ctx_raw.sem, 1)

                def ln_affine(b, n):
                    act.wait_ge(zt_acc.sem, zt_acc.at(layer, b, n + 1))
                    act.wait_ge(stored[n % 2].sem, stored[n % 2].at(layer, b, n // 2))
                    for ct in range(CT):
                        op = nc.scalar.activation(y_out[:, n % 2, columns_of(ct)], gen_ps[:, columns_of(ct)],
                                                  ACT.Identity, bias=cols[:, 5, ct:ct + 1], scale=cols[:, 4, ct:ct + 1])
                    op.then_inc(ln_done.sem, 1)

                def out_step(b, n):
                    if layer == 0 and n >= 2:
                        ln_affine(b, n - 2)

                def first_of(b, which):
                    for head in range(2):
                        if which == 1:
                            split_q(b, 0, head)
                        else:
                            split_k(b, 0, which // 2, head)

                def after_step(b, u, h):
                    if u + 1 < UNITS:
                        if h in (1, 2):
                            split_q(b, u + 1, h - 1)
                        if u % 2 == 0 and u // 2 + 1 < PAIRS:
                            if h in (6, 7):
                                split_k(b, u // 2 + 1, 0, h - 6)
                            if h in (12, 13):
                                split_k(b, u // 2 + 1, 1, h - 12)
                    if u % 2 == 1 and h in (3, 9):
                        split_w(b, 2 + u // 2, h // 9)
                    if u >= UNITS - 2 and h in (6, 10):
                        split_x(b + 1, 2 * (u - UNITS + 2) + h // 10)

                for k in range(2):
                    for which in range(2):
                        split_w(0, k, which)
                for ct in range(CT):
                    split_x(0, ct)
                act.wait_ge(wv_in_sem, 16 * (layer + 1))
                nc.scalar.activation(wv[:, 0, :, :], v[:, 0:CT, :], ACT.Copy).then_inc(wv_high, 1)
                act.wait_ge(prep_done, 2 * layer + 1)
                for which in range(3):
                    first_of(0, which)

                with act.Fori(0, B) as b:
                    split_max(b, 0)
                    for u in range(UNITS):
                        for h in range(STEPS):
                            exp_step(b, u, h)
                            if h == 0 and u > 0:
                                take_context(b, u - 1)
                            after_step(b, u, h)
                        if u + 1 < UNITS:
                            split_max(b, u + 1)
                    take_context(b, UNITS - 1)
                    for n in range(OUT_TILES + 2):
                        if n in FIRST_BEFORE:
                            first_of(b + 1, FIRST_BEFORE.index(n))
                        out_step(b, n)

        @block.vector
        def _(dve):
            dve.wait_ge(zeroed, 4)

            for layer in range(LAYERS):
                def split_w(b, k, which, layer=layer):
                    dve.wait_ge(w_high.sem, w_high.at(layer, b, 2 * k + which + 1))
                    nc.vector.scalar_tensor_tensor(
                        out=wqk[:, k % 2, which, 1, :], in0=wqk_raw[:, :], scalar=1.0 if which else QUERY_SCALE[layer],
                        in1=wqk[:, k % 2, which, 0, :].bitcast(F32), op0=ALU.mult, op1=ALU.subtract)\
                        .then_inc(w_low.sem, 1)

                def image_stats(b, ct, layer=layer):
                    dve.wait_ge(x_loaded[ct % 2].sem, x_loaded[ct % 2].at(layer, b, ct // 2 + 1))
                    for i in range(2):
                        op = nc.vector.bn_stats(bn[:, ct, 6 * i:6 * i + 6], x_in[:, ct % 2, columns_of(i, HALF)])
                    op.then_inc(bn_done.sem, 1)

                def group_deviation(b, layer=layer):
                    step = lambda k: dve.wait_ge(gn_step.sem, gn_step.at(layer, b, k))
                    dve.wait_ge(gn_mean_acc.sem, gn_mean_acc.at(layer, b, 1))
                    dve.wait_ge(gn_coef.sem, gn_coef.at(layer, b, 0))
                    nc.vector.tensor_reduce(g_mean[:, :], gen_ps[:, 0:CT * PARTS].rearrange("p (c g) -> p c g", g=PARTS),
                                            AX_X, ALU.add).then_inc(gn_step.sem, 1)
                    step(1)
                    for ct in range(CT):
                        op = nc.vector.tensor_scalar(g_dev[:, PARTS * ct:PARTS * ct + PARTS],
                                                     part_means[:, PARTS * ct:PARTS * ct + PARTS],
                                                     g_mean[:, ct:ct + 1], None, ALU.subtract)
                    op.then_inc(gn_step.sem, 1)
                    step(2)
                    nc.vector.tensor_tensor(g_sq[:, :], g_dev[:, :], g_dev[:, :], ALU.mult).then_inc(gn_step.sem, 1)
                    step(3)
                    nc.vector.scalar_tensor_tensor(out=g_exp[:, :], in0=part_squares, scalar=float(PARTS) / T,
                                                   in1=g_sq[:, :], op0=ALU.mult, op1=ALU.add).then_inc(gn_step.sem, 1)

                def group_variance(b, layer=layer):
                    dve.wait_ge(gn_var_acc.sem, gn_var_acc.at(layer, b, 1))
                    nc.vector.tensor_reduce(g_sum[:, :], gen_ps[:, 0:CT * PARTS].rearrange("p (c g) -> p c g", g=PARTS),
                                            AX_X, ALU.add).then_inc(gn_step.sem, 1)
                    dve.wait_ge(gn_step.sem, gn_step.at(layer, b, 5))
                    nc.vector.tensor_scalar(g_var[:, :], g_sum[:, :], EPS, None, ALU.add).then_inc(gn_step.sem, 1)

                def normalise(b, ct, layer=layer):
                    dve.wait_ge(x_loaded[ct % 2].sem, x_loaded[ct % 2].at(layer, b, 2 + ct // 2 + 1))
                    dve.wait_ge(gn_coef.sem, gn_coef.at(layer, b, 4))
                    nc.vector.tensor_scalar(x_in[:, ct % 2, :], x_in[:, ct % 2, :], g_scale[:, ct:ct + 1],
                                            g_shift[:, ct:ct + 1], ALU.mult, ALU.add).then_inc(x_norm.sem, 1)
                    dve.wait_ge(x_high.sem, x_high.at(layer, b, ct + 1))
                    nc.vector.tensor_tensor(xn[:, 1, ct, :], x_in[:, ct % 2, :], xn[:, 0, ct, :].bitcast(F32),
                                            ALU.subtract).then_inc(x_low.sem, 1)

                def split_k(b, pair, half, head):
                    own, ring, cs = OWN[head], pair % 2, columns_of(half, HALF)
                    dve.wait_ge(k_high.sem, k_high.at(layer, b, 4 * pair + 2 * half + head + 1))
                    nc.vector.scalar_tensor_tensor(
                        out=k_parts[OTHER[head], ring, head, cs], in0=k_ps[own, :],
                        scalar=bk[own, pair % PAIRS:pair % PAIRS + 1], in1=k_parts[own, ring, head, cs].bitcast(F32),
                        op0=ALU.add, op1=ALU.subtract).then_inc(k_low_done.sem, 1)

                def split_q(b, u, head):
                    own, ring, pair = OWN[head], u % 2, u // 2 % PAIRS
                    dve.wait_ge(q_high.sem, q_high.at(layer, b, 2 * u + head + 1))
                    nc.vector.scalar_tensor_tensor(
                        out=q_low[own, ring, head, :], in0=q_ps[own, :], scalar=bqs[own, pair:pair + 1],
                        in1=q_both[own, ring, head, :].bitcast(F32), op0=ALU.add, op1=ALU.subtract)\
                        .then_inc(q_low_done.sem, 1)

                def take_v(b, jt):
                    dve.wait_ge(v_acc.sem, v_acc.at(layer, b, jt + 1))
                    dve.wait_ge(pv_acc.sem, pv_acc.at(layer, b, 0))
                    nc.vector.tensor_tensor(v[:, jt, :], (q_ps, k_ps)[jt % 2][:, :], bias_rows[:, 0, :], ALU.add)\
                        .then_inc(v_done.sem, 1)

                def row_max(b, u, m):
                    it, head = m // 2, m % 2
                    dve.wait_ge(max_acc.sem, max_acc.at(layer, b, MAX_STEPS * u + m + 1))
                    if m == 0:
                        dve.wait_ge(mt_acc.sem, mt_acc.at(layer, b, u))
                    col = MAX_ROWS[head][0]
                    nc.vector.tensor_reduce(neg_max[:, it, col:col + 1], max_ps[:, :, :].rearrange("p a n -> p (a n)"),
                                            AX_X, ALU.max, negate=True).then_inc(max_done.sem, 1)

                def split_max(b, u):
                    for head in range(2):
                        dve.wait_ge(m_high.sem, m_high.at(layer, b, 2 * u + head + 1))
                        hi, lo = MAX_ROWS[head]
                        nc.vector.tensor_tensor(q_low[lo:lo + 1, u % 2, head, :], gen_ps[hi:hi + 1, :],
                                                q_low[hi:hi + 1, u % 2, head, :].bitcast(F32), ALU.subtract)\
                            .then_inc(m_low.sem, 1)

                def scale_context(b, u, part):
                    n = QUERY_TILES * u + part
                    if part == 0:
                        dve.wait_ge(l_acc.sem, l_acc.at(layer, b, u + 1))
                        dve.wait_ge(ctx_raw.sem, ctx_raw.at(layer, b, u + 1))
                    dve.wait_ge(ctx_done.sem, ctx_done.at(layer, b, max(n - 1, 0)))
                    nc.vector.reciprocal(inv_sum[:, part % 2, :], gen_ps[:, columns_of(part)]).then_inc(inv_done.sem, 1)
                    dve.wait_ge(inv_done.sem, inv_done.at(layer, b, n + 1))
                    context = heads_out[:, u // 2, columns_of(u % 2 * QUERY_TILES + part)]
                    nc.vector.tensor_tensor(context, context, inv_sum[:, part % 2, :], ALU.mult).then_inc(ctx_done.sem, 1)

                def out_token(b, n):
                    r = n % 2
                    dve.wait_ge(o_acc.sem, o_acc.at(layer, b, n + 1))
                    dve.wait_ge(zt_acc.sem, zt_acc.at(layer, b, max(n - 1, 0)))
                    nc.vector.tensor_tensor(y_tok[:, r, :], max_ps[:, r, :], bias_rows[:, 1, :], ALU.add)\
                        .then_inc(y_done.sem, 1)
                    dve.wait_ge(y_done.sem, y_done.at(layer, b, n + 1))
                    nc.vector.bn_stats(ln_bn[:, r, :], y_tok[:, r, :]).then_inc(ln_stat.sem, 1)
                    dve.wait_ge(ln_stat.sem, ln_stat.at(layer, b, 4 * n + 1))
                    halves = ln_bn[:, r, :].rearrange("p (g k) -> p k g", k=3)
                    nc.vector.tensor_reduce(ln_sums[:, r, :], halves[:, 1:3, :], AX_X, ALU.add)
                    nc.vector.tensor_tensor(ln_diff[:, r, :], ln_bn[:, r, 1:2], ln_bn[:, r, 4:5], ALU.subtract)\
                        .then_inc(ln_stat.sem, 1)
                    dve.wait_ge(ln_stat.sem, ln_stat.at(layer, b, 4 * n + 2))
                    nc.vector.tensor_scalar(ln_mean[:, r, :], ln_sums[:, r, 0:1], 0.5, None, ALU.mult)
                    nc.vector.tensor_scalar(ln_within[:, r, :], ln_sums[:, r, 1:2], 1.0 / C, EPS, ALU.mult, ALU.add)
                    nc.vector.scalar_tensor_tensor(out=ln_between[:, r, :], in0=ln_diff[:, r, :], scalar=0.25,
                                                   in1=ln_diff[:, r, :], op0=ALU.mult, op1=ALU.mult)\
                        .then_inc(ln_stat.sem, 1)
                    dve.wait_ge(ln_stat.sem, ln_stat.at(layer, b, 4 * n + 3))
                    dve.wait_ge(ln_pow.sem, ln_pow.at(layer, b, max(n - 1, 0)))
                    nc.vector.tensor_tensor(ln_var[:, r, :], ln_within[:, r, :], ln_between[:, r, :], ALU.add)\
                        .then_inc(ln_stat.sem, 1)

                def norm_token(b, n):
                    r = n % 2
                    dve.wait_ge(ln_pow.sem, ln_pow.at(layer, b, n + 1))
                    nc.vector.tensor_scalar(y_tok[:, r, :], y_tok[:, r, :], ln_mean[:, r, :], ln_rstd[:, r, :],
                                            ALU.subtract, ALU.mult).then_inc(z_done.sem, 1)

                def add_residual(b, n):
                    r = n % 2
                    dve.wait_ge(res_in[r].sem, res_in[r].at(layer, b, n // 2 + 1))
                    if layer == 0:
                        dve.wait_ge(ln_done.sem, ln_done.at(layer, b, n + 1))
                        nc.vector.tensor_tensor(y_out[:, r, :], y_out[:, r, :], x_res[:, r, :], ALU.add)\
                            .then_inc(out_done.sem, 1)
                    else:
                        dve.wait_ge(o_acc.sem, o_acc.at(layer, b, n + 1))
                        dve.wait_ge(stored[r].sem, stored[r].at(layer, b, n // 2))
                        nc.vector.scalar_tensor_tensor(out=y_out[:, r, :], in0=max_ps[:, r, :],
                                                       scalar=cols[:, 4, n % CT:n % CT + 1], in1=x_res[:, r, :],
                                                       op0=ALU.add, op1=ALU.add).then_inc(out_done.sem, 1)

                def out_step(b, n):
                    if layer == 1:
                        if n < OUT_TILES:
                            add_residual(b, n)
                        return
                    if n < OUT_TILES:
                        out_token(b, n)
                    if 1 <= n <= OUT_TILES:
                        norm_token(b, n - 1)
                    if n >= 2:
                        add_residual(b, n - 2)

                def first_of(b, which):
                    for head in range(2):
                        if which == 1:
                            split_q(b, 0, head)
                        else:
                            split_k(b, 0, which // 2, head)

                def after_step(b, u, h):
                    if u + 1 < UNITS:
                        if h in (2, 3):
                            split_q(b, u + 1, h - 2)
                        if h in MAX_AFTER:
                            row_max(b, u + 1, MAX_AFTER.index(h))
                        if u % 2 == 0 and u // 2 + 1 < PAIRS:
                            if h in (7, 8):
                                split_k(b, u // 2 + 1, 0, h - 7)
                            if h in (13, 14):
                                split_k(b, u // 2 + 1, 1, h - 13)
                    if u > 0 and SUM_AFTER < h <= SUM_AFTER + QUERY_TILES:
                        scale_context(b, u - 1, h - SUM_AFTER - 1)
                    if u % 2 == 1 and h in (3, 9):
                        split_w(b, 2 + u // 2, h // 9)
                    if u in (2, 3) and h in (1, 5):
                        image_stats(b + 1, 2 * (u - 2) + h // 5)
                    if (u, h) == (4, 12):
                        group_deviation(b + 1)
                    if (u, h) == (5, 13):
                        group_variance(b + 1)
                    if u >= UNITS - 2 and h in (6, 10):
                        normalise(b + 1, 2 * (u - UNITS + 2) + h // 10)

                dve.wait_ge(layer_in, 64 * (layer + 1))
                if layer:
                    dve.wait_ge(q_low_done.sem, q_low_done.at(layer, 0, 0))
                nc.vector.tensor_scalar(bqs[:, :], bq, QUERY_SCALE[layer], None, ALU.mult).then_inc(prep_done, 1)
                dve.wait_ge(prep_done, 2 * layer + 1)
                for ct in range(CT):
                    image_stats(0, ct)
                group_deviation(0)
                group_variance(0)
                for k in range(2):
                    for which in range(2):
                        split_w(0, k, which)
                for ct in range(CT):
                    normalise(0, ct)
                dve.wait_ge(wv_high, layer + 1)
                nc.vector.tensor_tensor(wv[:, 1, :, :], v[:, 0:CT, :], wv[:, 0, :, :].bitcast(F32), ALU.subtract)\
                    .then_inc(prep_done, 1)
                for which in range(3):
                    first_of(0, which)
                dve.wait_ge(prep_done, 2 * layer + 2)

                with dve.Fori(0, B) as b:
                    for jt in range(KT):
                        take_v(b, jt)
                        row_max(b, 0, jt)
                    split_max(b, 0)
                    for u in range(UNITS):
                        for h in range(STEPS):
                            after_step(b, u, h)
                        if u + 1 < UNITS:
                            split_max(b, u + 1)
                    for n in range(OUT_TILES + 2):
                        if n == 2:
                            for part in range(QUERY_TILES):
                                scale_context(b, UNITS - 1, part)
                        if n in FIRST_BEFORE:
                            first_of(b + 1, FIRST_BEFORE.index(n))
                        out_step(b, n)

        @block.gpsimd
        def _(pool):
            for counter in counts:
                pool.sem_inc(counter.sem, 1)
            nc.gpsimd.memset(k_ones.bitcast(F32), 0.0).then_inc(zeroed, 1)
            nc.gpsimd.memset(q_low[:, :, :, :].bitcast(F32), 0.0).then_inc(zeroed, 1)
            nc.gpsimd.memset(minus_half[:, :], -0.5)
            nc.gpsimd.memset(neg_max[:, :, :], 0.0).then_inc(zeroed, 1)
            pool.wait_ge(zeroed, 3)
            for head in range(2):
                for row in MAX_ROWS[head]:
                    op = nc.gpsimd.memset(k_ones[row:row + 1, :, head, :].bitcast(F32), 1.0)
            op.then_inc(zeroed, 1)
            pool.wait_ge(zeroed, 4)
            for layer in range(LAYERS):
                def coefficients(b, layer=layer):
                    step = lambda k: pool.wait_ge(gn_coef.sem, gn_coef.at(layer, b, k))
                    pool.wait_ge(gn_step.sem, gn_step.at(layer, b, 6))
                    pool.wait_ge(x_norm.sem, x_norm.at(layer, b, 0))
                    nc.gpsimd.tensor_tensor(g_rstd[:, :], g_var[:, :], minus_half[:, :], ALU.pow).then_inc(gn_coef.sem, 1)
                    step(1)
                    nc.gpsimd.tensor_tensor(g_scale[:, :], g_rstd[:, :], gamma, ALU.mult).then_inc(gn_coef.sem, 1)
                    step(2)
                    nc.gpsimd.tensor_tensor(g_tmp[:, :], g_mean[:, :], g_scale[:, :], ALU.mult).then_inc(gn_coef.sem, 1)
                    step(3)
                    nc.gpsimd.tensor_tensor(g_shift[:, :], beta, g_tmp[:, :], ALU.subtract).then_inc(gn_coef.sem, 1)

                def sum_step(b, u, h):
                    head, jt = h % 2, h // 2
                    total, new = e_sum[:, u % 2, head, :], e[:, h % RING, :]
                    if jt == 0:
                        return
                    pool.wait_ge(exp_done.sem, exp_done.at(layer, b, STEPS * u + h + 1))
                    if jt == 1:
                        pool.wait_ge(l_acc.sem, l_acc.at(layer, b, max(u - 1, 0)))
                        nc.gpsimd.tensor_tensor(total, e[:, head, :], new, ALU.add).then_inc(sum_done.sem, 1)
                    else:
                        pool.wait_ge(sum_done.sem, sum_done.at(layer, b, ADDS * u + 2 * (jt - 2) + head + 1))
                        nc.gpsimd.tensor_tensor(total, total, new, ALU.add).then_inc(sum_done.sem, 1)

                def out_step(b, n):
                    if layer == 0 and n < OUT_TILES:
                        r = n % 2
                        pool.wait_ge(ln_stat.sem, ln_stat.at(layer, b, 4 * n + 4))
                        pool.wait_ge(z_done.sem, z_done.at(layer, b, max(n - 1, 0)))
                        nc.gpsimd.tensor_tensor(ln_rstd[:, r, :], ln_var[:, r, :], minus_half[:, 0:1], ALU.pow)\
                            .then_inc(ln_pow.sem, 1)

                pool.wait_ge(layer_in, 64 * (layer + 1))
                coefficients(0)
                with pool.Fori(0, B) as b:
                    for u in range(UNITS):
                        for h in range(STEPS):
                            sum_step(b, u, h)
                            if (u, h) == (5, 14):
                                coefficients(b + 1)
                    for n in range(OUT_TILES):
                        out_step(b, n)


def kernel(**inputs):
    import numpy as np
    import concourse.bacc as bacc
    from concourse.bass_utils import run_bass_kernel_spmd

    def by_channel(vector):
        return vector.reshape(CT, P).T

    def transposed(w):
        return np.ascontiguousarray(w.T.reshape(CT, P, C).transpose(1, 0, 2))

    def by_pair(w):
        return w.reshape(PAIRS, P, CT, P).transpose(0, 3, 2, 1).reshape(PAIRS, P, CT * P)

    a = {name: np.asarray(value) for name, value in inputs.items()}
    x = a["x"].reshape(B, C, T)
    qkv_w, qkv_b = a["L1_conv_qkv_w"], a["L1_conv_qkv_b"]
    wq = [a["L0_conv_wq"], qkv_w[0:C]]
    wk = [a["L0_conv_wk"], qkv_w[C:2 * C]]
    wv = [a["L0_conv_wv"], qkv_w[2 * C:3 * C]]
    wo = [a["L0_conv_wo"], a["L1_conv_proj_w"]]
    per_channel = [
        [a["L0_conv_gn_gamma"], a["L0_conv_gn_beta"], a["L0_conv_bq"], a["L0_conv_bk"],
         a["L0_conv_ln_gamma"], a["L0_conv_ln_beta"]],
        [a["L1_conv_gn_scale"], a["L1_conv_gn_bias"], qkv_b[0:C], qkv_b[C:2 * C],
         a["L1_conv_proj_b"], a["L1_conv_proj_b"]],
    ]
    per_row = [[a["L0_conv_bv"], a["L0_conv_bo"]], [qkv_b[2 * C:3 * C], a["L1_conv_proj_b"]]]
    group = C // GROUPS
    constants = np.concatenate([
        np.eye(P, dtype=np.float32),
        np.kron(np.eye(P // group, dtype=np.float32), np.full((group, group), 1.0 / (group * PARTS), np.float32)),
        np.ones((P, D), np.float32),
    ], axis=1)

    arrays = {"in_x": x, "in_constants": constants}
    for layer in range(LAYERS):
        arrays[f"in_wqk{layer}"] = np.stack([by_pair(wq[layer]), by_pair(wk[layer])], axis=1)
        arrays[f"in_wv{layer}"] = transposed(wv[layer])
        arrays[f"in_wo{layer}"] = transposed(wo[layer])
        arrays[f"in_columns{layer}"] = np.stack([by_channel(c) for c in per_channel[layer]], axis=1)
        arrays[f"in_rows{layer}"] = np.stack(per_row[layer])
    arrays = {name: np.ascontiguousarray(value) for name, value in arrays.items()}

    nc = bacc.Bacc("TRN2", target_bir_lowering=False, num_devices=1)
    dram = {name: nc.dram_tensor(name, value.shape, F32, kind="ExternalInput").ap() for name, value in arrays.items()}
    middle = nc.dram_tensor("middle", [B, C, T], F32).ap()
    out = nc.dram_tensor("out", [B, C, T], F32, kind="ExternalOutput").ap()
    attention_blocks(nc, dram["in_x"], out, middle, [dram[f"in_wqk{i}"] for i in range(LAYERS)],
                     [dram[f"in_wv{i}"] for i in range(LAYERS)], [dram[f"in_wo{i}"] for i in range(LAYERS)],
                     [dram[f"in_columns{i}"] for i in range(LAYERS)], [dram[f"in_rows{i}"] for i in range(LAYERS)],
                     dram["in_constants"])
    result = run_bass_kernel_spmd(nc, [arrays], core_ids=[0])
    return result.results[0]["out"].reshape(B, C, 32, 32)
```

```python
from contextlib import ExitStack

import concourse.bass as bass
from concourse import mybir

F32 = mybir.dt.float32
F32R = mybir.dt.float32r
ALU = mybir.AluOpType
ACT = mybir.ActivationFunctionType
AX_X = mybir.AxisListType.X

P = 128
B, C, T = 8, 512, 1024
HEADS, D = 8, 64
GROUPS = 32
EPS = 1e-5
CT = C // P
PAIRS = HEADS // 2
HALF = T // 2
UNITS = 2 * PAIRS
KT = T // P
STEPS = 2 * KT
RING = 8
ADDS = 2 * (KT - 1)
MAX_STEPS = 2 * 2 * HALF // P
MAX_HALF = MAX_STEPS // 2
MAX_AFTER = ((0, 0, 0, 0, 1, 3, 1, 1, 1, 2, 1, 2, 1, 2, 1, 0),
             (0, 0, 0, 0, 1, 3, 1, 1, 1, 2, 1, 2, 1, 2, 1, 0))
K_AFTER = (2, 18)
K_HIGH_AFTER = ((5, 6), (21, 22))
K_LOW_AFTER = ((6, 7), (22, 23))
Q_HIGH_AFTER = (1, 2)
Q_LOW_AFTER = (2, 3)
W_HIGH_AFTER = 10
W_LOW_AFTER = 11
STATS_AFTER = (0, 1)
CONTEXT_AFTER = 0
SUM_AFTER = 9
SCALE_AFTER = ((10, 12, 15, 16), (16, 17, 18, 19), (10, 11, 12, 13), (0, 0, 0, 1))
FIRST_BEFORE = (5, 6, 7, 8, 9)
NORMALISE_AFTER = ((6, 6), (6, 7), (7, 4), (7, 7))
SPLIT_X_AFTER = ((6, 8), (6, 10), (7, 6), (7, 12))
LOW_X_AFTER = ((6, 14), (7, 0), (7, 8), (7, 14))
QUERY_TILES = HALF // P
OUT_TILES = 8
LAYERS = 2
PARTS = 4
QUERY_SCALE = (float(D) ** -0.25, float(D) ** -0.5)


def max_steps_after(u, h):
    after = MAX_AFTER[u % 2]
    return range(sum(after[:h]), sum(after[:h + 1]))


def k_splits(u, h, after):
    at = h + STEPS * (u % 2)
    return [(half, head) for half in range(2) for head in range(2) if at == after[half][head] and u < UNITS - 2]


def scales(u, h):
    for unit in range(max(u - 2, 0), u):
        for part, at in enumerate(SCALE_AFTER[max(unit - (UNITS - 4), 0)]):
            if h + STEPS * (u - unit - 1) == at:
                yield unit, part


def v_chunks_after(m):
    quarters = CT * (KT - 2)
    start, end = (quarters * i // (MAX_STEPS + 2) for i in (m, m + 1))
    return range(start, quarters if m == MAX_STEPS - 1 else end)


class Count:

    def __init__(self, sem, per_image, ahead=0, by=1):
        self.sem, self.per_image, self.ahead, self.by = sem, per_image, ahead, by

    def at(self, layer, b, k):
        return (layer * (B * self.per_image + self.ahead) + k) * self.by + 1 + b * (self.per_image * self.by)


def attention_blocks(nc, x, out, middle, weights, wv_in, wo_in, columns, rows, constants):
    with ExitStack() as ctx_:
        def sb(name, shape, dt=F32):
            return ctx_.enter_context(nc.sbuf_tensor(name, shape, dt))

        def psum(name, shape):
            return ctx_.enter_context(nc.psum_tensor(name, shape, F32))

        def sem(name):
            return ctx_.enter_context(nc.semaphore(name))

        counts = []

        def count(name, per_image, ahead=0, by=1):
            counts.append(Count(sem(name), per_image, ahead, by))
            return counts[-1]

        consts = sb("consts", [P, 2 * P + D])
        identity, group_mean, ones = consts[:, 0:P], consts[:, P:2 * P], consts[:, 2 * P:2 * P + D]
        cols = sb("cols", [P, 6, CT])
        gamma, beta, bq, bk = (cols[:, i, :] for i in range(4))
        bias_rows = sb("bias_rows", [P, 2, C])
        bqs = sb("bqs", [P, CT])
        wv = sb("wv", [P, 2, CT, C], F32R)
        wo = sb("wo", [P, CT, C])
        wqk_raw = sb("wqk_raw", [P, CT * P])
        wqk = sb("wqk", [P, 2, 2, 2, CT * P], F32R)
        x_in = sb("x_in", [P, 2, T])
        xn = sb("xn", [P, 2, CT, T], F32R)
        q_both = sb("q_both", [P, 2, 2, HALF], F32R)
        q_low = sb("q_low", [P, 2, 2, HALF], F32R)
        k_sets = sb("k_sets", [P, 2, 2, 2, T], F32R)
        k_parts, k_ones = k_sets[:, 0], k_sets[:, 1]
        v = sb("v", [P, KT, C])
        e = sb("e", [P, RING, HALF])
        e_sum = sb("e_sum", [P, 2, 2, HALF])
        inv_sum = sb("inv_sum", [P, 2, P])
        neg_max = sb("neg_max", [P, QUERY_TILES, D + 1])
        half_max = sb("half_max", [P, 2, QUERY_TILES, 2])
        heads_out = sb("heads_out", [P, CT, T])
        x_res = sb("x_res", [P, 2, HALF])
        y_out = sb("y_out", [P, 2, HALF])
        y_tok = sb("y_tok", [P, 2, C])
        bn = sb("bn", [P, CT, 3 * PARTS])
        part_means, part_squares = (bn[:, :, :].rearrange("p c (g k) -> p (c g) k", k=3)[:, :, i] for i in (1, 2))
        g_mean = sb("g_mean", [P, CT])
        g_dev = sb("g_dev", [P, CT * PARTS])
        g_sq = sb("g_sq", [P, CT * PARTS])
        g_exp = sb("g_exp", [P, CT * PARTS])
        g_sum = sb("g_sum", [P, CT])
        g_var = sb("g_var", [P, CT])
        g_rstd = sb("g_rstd", [P, CT])
        g_scale = sb("g_scale", [P, CT])
        g_tmp = sb("g_tmp", [P, CT])
        g_shift = sb("g_shift", [P, CT])
        minus_half = sb("minus_half", [P, CT])
        ln_bn = sb("ln_bn", [P, 2, 6])
        ln_sums = sb("ln_sums", [P, 2, 2])
        ln_diff = sb("ln_diff", [P, 2, 1])
        ln_mean = sb("ln_mean", [P, 2, 1])
        ln_within = sb("ln_within", [P, 2, 1])
        ln_between = sb("ln_between", [P, 2, 1])
        ln_var = sb("ln_var", [P, 2, 1])
        ln_rstd = sb("ln_rstd", [P, 2, 1])

        scores_ps = psum("scores_ps", [P, 2, HALF])
        max_ps = psum("max_ps", [P, 2, HALF])
        acc_ps = psum("acc_ps", [P, HALF])
        q_ps = psum("q_ps", [P, HALF])
        k_ps = psum("k_ps", [P, HALF])
        gen_ps = psum("gen_ps", [P, HALF])

        max_banks = (max_ps[:, 0, :], max_ps[:, 1, :], gen_ps[:, :])

        k_acc = count("k_acc", 2 * PAIRS, 2)
        q_acc = count("q_acc", UNITS, 1)
        v_acc = count("v_acc", KT, 2)
        max_acc = count("max_acc", MAX_STEPS * UNITS)
        mt_acc = count("mt_acc", UNITS)
        s_acc = count("s_acc", STEPS * UNITS)
        pv_acc = count("pv_acc", KT * UNITS)
        l_acc = count("l_acc", UNITS)
        o_acc = count("o_acc", OUT_TILES)
        gn_mean_acc = count("gn_mean_acc", 1, 1)
        gn_var_acc = count("gn_var_acc", 1, 1)
        zt_acc = count("zt_acc", OUT_TILES)
        w_high = count("w_high", 2 * PAIRS, 3)
        k_high = count("k_high", 4 * PAIRS, 4)
        q_high = count("q_high", 2 * UNITS, 2)
        m_high = count("m_high", 2 * UNITS)
        exp_done = count("exp_done", STEPS * UNITS)
        x_high = count("x_high", CT, CT)
        ctx_raw = count("ctx_raw", UNITS)
        ln_done = count("ln_done", OUT_TILES)
        wv_high = sem("wv_high")
        w_low = count("w_low", 2 * PAIRS, 3)
        k_low_done = count("k_low_done", 4 * PAIRS, 4)
        q_low_done = count("q_low_done", 2 * UNITS, 2)
        m_low = count("m_low", 2 * UNITS)
        max_done = count("max_done", MAX_STEPS * UNITS)
        max_both = count("max_both", UNITS)
        v_done = count("v_done", KT, 2)
        inv_done = count("inv_done", QUERY_TILES * UNITS)
        ctx_done = count("ctx_done", QUERY_TILES * UNITS)
        bn_done = count("bn_done", CT, CT)
        gn_step = count("gn_step", 6, 6)
        x_norm = count("x_norm", CT, CT)
        x_low = count("x_low", CT, CT)
        y_done = count("y_done", OUT_TILES)
        ln_stat = count("ln_stat", 4 * OUT_TILES)
        z_done = count("z_done", OUT_TILES)
        out_done = count("out_done", OUT_TILES)
        prep_done = sem("prep_done")
        zeroed = sem("zeroed")
        sum_done = count("sum_done", ADDS * UNITS)
        gn_coef = count("gn_coef", 4, 4)
        ln_pow = count("ln_pow", OUT_TILES)
        setup_in = sem("setup_in")
        layer_in = sem("layer_in")
        cols_in = sem("cols_in")
        first_x_in = [sem(f"first_x_in{ct}") for ct in range(CT)]
        wv_in_sem = sem("wv_in_sem")
        w_in = count("w_in", 2 * PAIRS, 3, by=16)
        x_loaded = [count(f"x_loaded{i}", CT, by=16) for i in range(2)]
        res_in = [count(f"res_in{i}", OUT_TILES // 2, by=16) for i in range(2)]
        stored = [count(f"stored{i}", OUT_TILES // 2, by=16) for i in range(2)]

        block = ctx_.enter_context(nc.Block())
        LOW, TOP = slice(0, D), slice(D, P)
        OWN = (LOW, TOP)
        OTHER = (TOP, LOW)
        MAX_ROWS = ((D, D + 32), (0, 32))

        def columns_of(tile, n=P):
            return slice(tile * n, (tile + 1) * n)

        @block.sync
        def _(sp):
            sp.dma_start(consts[:], constants).then_inc(setup_in, 16)
            for layer in range(LAYERS):
                source = x if layer == 0 else middle
                target = middle if layer == 0 else out

                def load_stats(gi_b, img, ct, layer=layer, source=source):
                    if ct < 2:
                        sp.wait_ge(x_low.sem, x_low.at(layer, gi_b, 0))
                    else:
                        sp.wait_ge(bn_done.sem, bn_done.at(layer, gi_b, ct - 1))
                    sp.dma_start(x_in[:, ct % 2, :], source[img, columns_of(ct), :])\
                        .then_inc(x_loaded[ct % 2].sem, 16)

                def load_norm(gi_b, img, ct, layer=layer, source=source):
                    if ct < 2:
                        sp.wait_ge(bn_done.sem, bn_done.at(layer, gi_b, ct + 3))
                    else:
                        sp.wait_ge(x_low.sem, x_low.at(layer, gi_b, ct - 1))
                    sp.dma_start(x_in[:, ct % 2, :], source[img, columns_of(ct), :])\
                        .then_inc(x_loaded[ct % 2].sem, 16)

                def load_w(b, i, layer=layer):
                    sp.wait_ge(w_high.sem, w_high.at(layer, b, i))
                    sp.wait_ge(w_low.sem, w_low.at(layer, b, i))
                    sp.dma_start(wqk_raw[:, :], weights[layer][i // 2 % PAIRS, 1 - i % 2]).then_inc(w_in.sem, 16)

                if layer:
                    sp.wait_ge(o_acc.sem, o_acc.at(layer, 0, 0))
                    for ring in range(2):
                        sp.wait_ge(stored[ring].sem, stored[ring].at(layer - 1, 1, 0))
                load_w(0, 0)
                for ct in range(CT):
                    sp.dma_start(heads_out[:, ct, :], source[0, columns_of(ct), :]).then_inc(first_x_in[ct], 16)
                if layer:
                    for ring in range(2):
                        sp.wait_ge(stored[ring].sem, stored[ring].at(layer, 0, 0))
                    sp.wait_ge(k_low_done.sem, k_low_done.at(layer, 0, 0))
                    sp.wait_ge(v_done.sem, v_done.at(layer, 0, 0))
                sp.dma_start(cols[:, :, :], columns[layer]).then_inc(cols_in, 16)
                for i in range(1, 3):
                    load_w(0, i)
                sp.dma_start(v[:, 0:CT, :], wv_in[layer]).then_inc(wv_in_sem, 16)
                for i in range(2):
                    sp.dma_start(bias_rows[:, i, :], rows[layer][i:i + 1, :].broadcast_to([P, C])).then_inc(layer_in, 16)
                sp.dma_start(wo[:, :, :], wo_in[layer]).then_inc(layer_in, 16)

                with sp.Fori(0, B) as b:
                    nxt = (b + 1) % B
                    load_w(b, 3)
                    load_stats(b + 1, nxt, 0)
                    load_stats(b + 1, nxt, 1)
                    load_w(b, 4)
                    load_stats(b + 1, nxt, 2)
                    load_w(b, 5)
                    load_stats(b + 1, nxt, 3)
                    load_w(b, 6)
                    load_norm(b + 1, nxt, 0)
                    load_w(b, 7)
                    load_norm(b + 1, nxt, 1)
                    load_w(b, 8)
                    load_w(b, 9)
                    load_w(b, 10)

                    def load_res(n):
                        sp.wait_ge(out_done.sem, out_done.at(layer, b, max(n - 1, 0)))
                        if layer == 0:
                            src = source[b].rearrange("(c p) t -> p c t", p=P)[:, :, columns_of(n)]
                            dst = x_res[:, n % 2, :].rearrange("p (c t) -> p c t", c=CT)
                        else:
                            src = source[b, columns_of(n % CT), columns_of(n // CT, HALF)]
                            dst = x_res[:, n % 2, :]
                        sp.dma_start(dst, src).then_inc(res_in[n % 2].sem, 16)

                    load_res(0)
                    load_res(1)
                    load_norm(b + 1, nxt, 2)
                    load_norm(b + 1, nxt, 3)
                    for n in range(OUT_TILES):
                        sp.wait_ge(out_done.sem, out_done.at(layer, b, n + 1))
                        if layer == 0:
                            dst = target[b].rearrange("(c p) t -> p c t", p=P)[:, :, columns_of(n)]
                            src = y_out[:, n % 2, :].rearrange("p (c t) -> p c t", c=CT)
                        else:
                            dst = target[b, columns_of(n % CT), columns_of(n // CT, HALF)]
                            src = y_out[:, n % 2, :]
                        sp.dma_start(dst, src).then_inc(stored[n % 2].sem, 16)
                        if n + 2 < OUT_TILES:
                            load_res(n + 2)
            for ring in range(2):
                sp.wait_ge(stored[ring].sem, stored[ring].at(LAYERS, 0, 0))

        @block.tensor
        def _(pe):
            pe.wait_ge(setup_in, 16)
            for layer in range(LAYERS):
                gen_reader = []

                def fill_gen(*readers):
                    for counter, value in gen_reader:
                        pe.wait_ge(counter.sem, value)
                    gen_reader[:] = readers

                def group_means(b, layer=layer):
                    pe.wait_ge(bn_done.sem, bn_done.at(layer, b, CT))
                    fill_gen((gn_step, gn_step.at(layer, b, 1)))
                    pe.matmul(gen_ps[:, 0:CT * PARTS], group_mean, part_means, start=True, stop=True)\
                        .then_inc(gn_mean_acc.sem, 1)

                def group_vars(b, layer=layer):
                    pe.wait_ge(gn_step.sem, gn_step.at(layer, b, 4))
                    fill_gen((gn_step, gn_step.at(layer, b, 5)))
                    pe.matmul(gen_ps[:, 0:CT * PARTS], group_mean, g_exp[:, :], start=True, stop=True)\
                        .then_inc(gn_var_acc.sem, 1)

                def project(dst, which, pair, half, b, chunks, ready):
                    for kt in chunks:
                        for n, (w_part, x_part) in enumerate(((0, 0), (0, 1), (1, 0))):
                            mm = pe.matmul(dst, wqk[:, pair % 2, which, w_part, columns_of(kt)],
                                           xn[:, x_part, kt, columns_of(half, HALF)],
                                           start=kt == 0 and n == 0, stop=kt == CT - 1 and n == 2)
                        if kt == CT - 1:
                            mm.then_inc(ready.sem, 1)

                def k_tile(b, pair, half, chunks=range(CT)):
                    if chunks[0] == 0:
                        pe.wait_ge(w_high.sem, w_high.at(layer, b, 2 * pair + 1))
                        pe.wait_ge(w_low.sem, w_low.at(layer, b, 2 * pair + 1))
                        if (pair, half) == (1, 0):
                            pe.wait_ge(v_done.sem, v_done.at(layer, b, KT))
                        pe.wait_ge(inv_done.sem, inv_done.at(layer, b, QUERY_TILES * max(2 * pair - 3 + half, 0)))
                        pe.wait_ge(k_low_done.sem, k_low_done.at(layer, b, 4 * pair + 2 * half))
                        pe.wait_ge(k_high.sem, k_high.at(layer, b, 4 * pair + 2 * half))
                    project(k_ps[:, :], 1, pair, half, b, chunks, k_acc)

                def q_tile(b, u, chunks=range(CT)):
                    if chunks[0] == 0:
                        pe.wait_ge(w_high.sem, w_high.at(layer, b, 2 * (u // 2) + 2))
                        pe.wait_ge(w_low.sem, w_low.at(layer, b, 2 * (u // 2) + 2))
                        if u == 1:
                            pe.wait_ge(v_done.sem, v_done.at(layer, b, KT - 1))
                        pe.wait_ge(q_low_done.sem, q_low_done.at(layer, b, 2 * u))
                        pe.wait_ge(q_high.sem, q_high.at(layer, b, 2 * u))
                    project(q_ps[:, :], 0, u // 2, u % 2, b, chunks, q_acc)

                def v_tile(b, jt, chunks=range(CT)):
                    dst = (q_ps, k_ps)[jt % 2]
                    if chunks[0]:
                        pass
                    elif jt >= 2:
                        pe.wait_ge(v_done.sem, v_done.at(layer, b, jt - 1))
                    elif jt == 0:
                        pe.wait_ge(q_high.sem, q_high.at(layer, b, 2))
                        pe.wait_ge(q_low_done.sem, q_low_done.at(layer, b, 2))
                    else:
                        pe.wait_ge(k_high.sem, k_high.at(layer, b, 4))
                        pe.wait_ge(k_low_done.sem, k_low_done.at(layer, b, 4))
                    for kt in chunks:
                        for n, (x_part, w_part) in enumerate(((0, 0), (0, 1), (1, 0))):
                            mm = pe.matmul(dst[:, :], xn[:, x_part, kt, columns_of(jt)], wv[:, w_part, kt, :],
                                           start=kt == 0 and n == 0, stop=kt == CT - 1 and n == 2)
                    if kt == CT - 1:
                        mm.then_inc(v_acc.sem, 1)

                def max_step(b, u, m):
                    half, it, head = m // MAX_HALF, m // 2 % QUERY_TILES, m % 2
                    if m < 2:
                        pe.wait_ge(q_high.sem, q_high.at(layer, b, 2 * u + head + 1))
                    if m % MAX_HALF == 0:
                        pe.wait_ge(k_high.sem, k_high.at(layer, b, 4 * (u // 2) + 2 * half + 2))
                        pe.wait_ge(k_low_done.sem, k_low_done.at(layer, b, 4 * (u // 2) + 2 * half + 2))
                    pe.wait_ge(max_done.sem, max_done.at(layer, b, MAX_STEPS * u + max(m - 2, 0)))
                    if m % 3 == 2:
                        fill_gen((max_done, max_done.at(layer, b, MAX_STEPS * u + m + 1)))
                    pe.matmul(max_banks[m % 3], q_both[:, u % 2, head, columns_of(it)],
                              k_parts[:, u // 2 % 2, head, columns_of(half, HALF)], start=True, stop=True)\
                        .then_inc(max_acc.sem, 1)

                def max_rows(b, u):
                    pe.wait_ge(max_both.sem, max_both.at(layer, b, u + 1))
                    fill_gen((m_high, m_high.at(layer, b, 2 * u + 2)), (m_low, m_low.at(layer, b, 2 * u + 2)))
                    for it in range(QUERY_TILES):
                        mm = pe.transpose(gen_ps[0:D + 1, columns_of(it)], neg_max[:, it, :], identity)
                    mm.then_inc(mt_acc.sem, 1)

                def score_step(b, u, h):
                    head, ring, keys = h % 2, u % 2, columns_of(h // 2)
                    if h < 2:
                        pe.wait_ge(m_high.sem, m_high.at(layer, b, 2 * u + h + 1))
                        pe.wait_ge(m_low.sem, m_low.at(layer, b, 2 * u + h + 1))
                        pe.wait_ge(q_low_done.sem, q_low_done.at(layer, b, 2 * u + h + 1))
                    pe.wait_ge(exp_done.sem, exp_done.at(layer, b, max(STEPS * u + h - 1, 0)))
                    pe.matmul(scores_ps[:, h % 2, :], k_parts[:, u // 2 % 2, head, keys],
                              q_both[:, ring, head, :], start=True, stop=False)
                    pe.matmul(scores_ps[:, h % 2, :], k_ones[:, u // 2 % 2, head, keys],
                              q_low[:, ring, head, :], start=False, stop=True).then_inc(s_acc.sem, 1)

                def value_step(b, u, jt):
                    pe.wait_ge(exp_done.sem, exp_done.at(layer, b, STEPS * u + 2 * jt + 2))
                    if jt == 0:
                        if u == 0:
                            pe.wait_ge(v_done.sem, v_done.at(layer, b, KT))
                        pe.wait_ge(ctx_raw.sem, ctx_raw.at(layer, b, u))
                    for head in range(2):
                        at = (2 * (u // 2) + head) * D
                        mm = pe.matmul(acc_ps[OWN[head], :], v[:, jt, at:at + D],
                                       e[:, (2 * jt + head) % RING, :], start=jt == 0, stop=jt == KT - 1)
                    mm.then_inc(pv_acc.sem, 1)

                def sum_step(b, u):
                    pe.wait_ge(sum_done.sem, sum_done.at(layer, b, ADDS * (u + 1)))
                    split = min(2 * u + 8, 4 * PAIRS)
                    pe.wait_ge(k_high.sem, k_high.at(layer, b, split))
                    pe.wait_ge(k_low_done.sem, k_low_done.at(layer, b, split))
                    for head in range(2):
                        mm = pe.matmul(k_ps[OWN[head], :], ones, e_sum[:, u % 2, head, :], start=True, stop=True)
                    mm.then_inc(l_acc.sem, 1)

                def out_tile(b, n):
                    pe.wait_ge(ctx_done.sem, ctx_done.at(layer, b, QUERY_TILES * (UNITS - 1 + n // 4)))
                    if n < 2:
                        pe.wait_ge(max_done.sem, max_done.at(layer, b, MAX_STEPS * UNITS))
                    else:
                        reader = y_done if layer == 0 else out_done
                        pe.wait_ge(reader.sem, reader.at(layer, b, n - 1))
                    for kt in range(CT):
                        if layer == 0:
                            lhs, rhs = heads_out[:, kt, columns_of(n)], wo[:, kt, :]
                        else:
                            lhs, rhs = wo[:, kt, columns_of(n % CT)], heads_out[:, kt, columns_of(n // CT, HALF)]
                        mm = pe.matmul(max_ps[:, n % 2, :], lhs, rhs, start=kt == 0, stop=kt == CT - 1)
                    mm.then_inc(o_acc.sem, 1)

                def token_turn(b, n):
                    pe.wait_ge(z_done.sem, z_done.at(layer, b, n + 1))
                    fill_gen((ln_done, ln_done.at(layer, b, n + 1)))
                    for ct in range(CT):
                        mm = pe.transpose(gen_ps[:, columns_of(ct)], y_tok[:, n % 2, columns_of(ct)], identity)
                    mm.then_inc(zt_acc.sem, 1)

                def out_step(b, n):
                    if n < OUT_TILES:
                        out_tile(b, n)
                    if layer == 0 and n >= 2:
                        token_turn(b, n - 2)

                if layer:
                    gen_reader[:] = [(ln_done, ln_done.at(1, 0, 0))]
                group_means(0)
                group_vars(0)
                pe.wait_ge(zeroed, 4)

                def first_of(b, which):
                    if which == 0:
                        for ct in range(CT):
                            pe.wait_ge(x_high.sem, x_high.at(layer, b, ct + 1))
                            pe.wait_ge(x_low.sem, x_low.at(layer, b, ct + 1))
                            k_tile(b, 0, 0, (ct,))
                    elif which == 1:
                        q_tile(b, 0)
                    elif which == 2:
                        k_tile(b, 0, 1)
                    else:
                        v_tile(b, which - 3)

                for which in range(5):
                    if which == 3:
                        pe.wait_ge(wv_high, layer + 1)
                        pe.wait_ge(prep_done, 2 * (layer + 1))
                    first_of(0, which)
                pe.wait_ge(layer_in, 48 * (layer + 1))

                with pe.Fori(0, B) as b:
                    gen_reader[:] = [(gn_step, gn_step.at(layer, b, 6))]
                    if layer == 0:
                        gen_reader.append((ln_done, ln_done.at(layer, b, 0)))
                    last_out = y_done if layer == 0 else out_done
                    pe.wait_ge(last_out.sem, last_out.at(layer, b, 0))
                    for m in range(MAX_STEPS):
                        max_step(b, 0, m)
                        for chunk in v_chunks_after(m):
                            v_tile(b, 2 + chunk // CT, (chunk % CT,))
                    max_rows(b, 0)
                    q_tile(b, 1, (0, 1))
                    for u in range(UNITS):
                        last = u == UNITS - 1
                        for h in range(STEPS):
                            score_step(b, u, h)
                            if not last:
                                for m in max_steps_after(u, h):
                                    max_step(b, u + 1, m)
                            if h >= 4 and h % 2 == 0:
                                value_step(b, u, h // 2 - 2)
                            if h == STEPS - 1:
                                value_step(b, u, KT - 2)
                            if not last:
                                if h < 2:
                                    q_tile(b, u + 1, (h + 2,))
                                for half in range(2):
                                    chunk = h + STEPS * (u % 2) - K_AFTER[half]
                                    if 0 <= chunk < CT and u < UNITS - 2:
                                        k_tile(b, u // 2 + 1, half, (chunk,))
                            if h == SUM_AFTER and u > 0 and u != UNITS - 2:
                                sum_step(b, u - 1)
                            if (u, h) == (4, 1):
                                group_means(b + 1)
                            if (u, h) == (5, 1):
                                group_vars(b + 1)
                        if u + 2 < UNITS:
                            q_tile(b, u + 2, (0,))
                        if not last:
                            max_rows(b, u + 1)
                        else:
                            out_step(b, 0)
                        value_step(b, u, KT - 1)
                        if u + 2 < UNITS:
                            q_tile(b, u + 2, (1,))
                        elif not last:
                            sum_step(b, u - 1)
                    for n in range(1, OUT_TILES + 2):
                        if n == 1:
                            sum_step(b, UNITS - 1)
                        if n in FIRST_BEFORE:
                            first_of(b + 1, FIRST_BEFORE.index(n))
                        out_step(b, n)

        @block.scalar
        def _(act):
            for layer in range(LAYERS):
                def split_w(b, i, layer=layer):
                    pair, which = i // 2, 1 - i % 2
                    act.wait_ge(w_in.sem, w_in.at(layer, b, i + 1))
                    user = k_acc if which else q_acc
                    act.wait_ge(user.sem, user.at(layer, b, max(2 * (pair - 1), 0)))
                    nc.scalar.activation(wqk[:, pair % 2, which, 0, :], wqk_raw[:, :], ACT.Copy,
                                         scale=1.0 if which else QUERY_SCALE[layer]).then_inc(w_high.sem, 1)

                def split_x(b, ct, layer=layer, first=False):
                    act.wait_ge(q_acc.sem, q_acc.at(layer, b, 0))
                    act.wait_ge(k_acc.sem, k_acc.at(layer, b, 0))
                    act.wait_ge(x_norm.sem, x_norm.at(layer, b, ct + 1))
                    tile = heads_out[:, ct, :] if first else x_in[:, ct % 2, :]
                    nc.scalar.activation(xn[:, 0, ct, :], tile, ACT.Copy).then_inc(x_high.sem, 1)

                def split_k(b, pair, half, head):
                    own, ring = OWN[head], pair % 2
                    act.wait_ge(k_acc.sem, k_acc.at(layer, b, 2 * pair + half + 1))
                    act.wait_ge(s_acc.sem, s_acc.at(layer, b, max(2 * STEPS * (pair - 1), 0)))
                    both = k_ps[own, :].rearrange("p (a n) -> p a n", a=1).broadcast_to([D, 2, HALF])
                    nc.scalar.activation(k_sets[own, :, ring, head, columns_of(half, HALF)], both,
                                         ACT.Identity, bias=bk[own, pair % PAIRS:pair % PAIRS + 1]).then_inc(k_high.sem, 1)

                def split_q(b, u, head):
                    own, ring, pair = OWN[head], u % 2, u // 2 % PAIRS
                    act.wait_ge(q_acc.sem, q_acc.at(layer, b, u + 1))
                    act.wait_ge(s_acc.sem, s_acc.at(layer, b, max(STEPS * (u - 1), 0)))
                    for place in (own, OTHER[head]):
                        op = nc.scalar.activation(q_both[place, ring, head, :], q_ps[own, :],
                                                  ACT.Identity, bias=bqs[own, pair:pair + 1])
                    op.then_inc(q_high.sem, 1)

                def split_max(b, u):
                    act.wait_ge(mt_acc.sem, mt_acc.at(layer, b, u + 1))
                    act.wait_ge(s_acc.sem, s_acc.at(layer, b, max(STEPS * (u - 1), 0)))
                    for head in range(2):
                        row = MAX_ROWS[head][0]
                        nc.scalar.activation(q_low[row:row + 1, u % 2, head, :], gen_ps[row:row + 1, :], ACT.Copy)\
                            .then_inc(m_high.sem, 1)

                def exp_step(b, u, h):
                    act.wait_ge(s_acc.sem, s_acc.at(layer, b, STEPS * u + h + 1))
                    old_u, old_h = divmod(STEPS * u + h - RING, STEPS)
                    used = KT * old_u + old_h // 2 + 1 if old_u >= 0 else 0
                    added = ADDS * old_u + 2 * max(old_h // 2 - 1, 0) + old_h % 2 + 1 if old_u >= 0 else 0
                    act.wait_ge(pv_acc.sem, pv_acc.at(layer, b, used))
                    act.wait_ge(sum_done.sem, sum_done.at(layer, b, added))
                    nc.scalar.activation(e[:, h % RING, :], scores_ps[:, h % 2, :], ACT.Exp).then_inc(exp_done.sem, 1)

                def take_context(b, u):
                    act.wait_ge(pv_acc.sem, pv_acc.at(layer, b, KT * (u + 1)))
                    if u < 2:
                        act.wait_ge(o_acc.sem, o_acc.at(layer, b, 0))
                    nc.scalar.activation(heads_out[:, u // 2, columns_of(u % 2, HALF)], acc_ps[:, :], ACT.Copy)\
                        .then_inc(ctx_raw.sem, 1)

                def ln_affine(b, n):
                    act.wait_ge(zt_acc.sem, zt_acc.at(layer, b, n + 1))
                    act.wait_ge(stored[n % 2].sem, stored[n % 2].at(layer, b, n // 2))
                    for ct in range(CT):
                        op = nc.scalar.activation(y_out[:, n % 2, columns_of(ct)], gen_ps[:, columns_of(ct)],
                                                  ACT.Identity, bias=cols[:, 5, ct:ct + 1], scale=cols[:, 4, ct:ct + 1])
                    op.then_inc(ln_done.sem, 1)

                def out_step(b, n):
                    if layer == 0 and n >= 2:
                        ln_affine(b, n - 2)

                def first_of(b, which):
                    for head in range(2 if which < 3 else 0):
                        if which == 1:
                            split_q(b, 0, head)
                        else:
                            split_k(b, 0, which // 2, head)

                def after_step(b, u, h):
                    if u + 1 < UNITS and h in Q_HIGH_AFTER:
                        split_q(b, u + 1, Q_HIGH_AFTER.index(h))
                    for half, head in k_splits(u, h, K_HIGH_AFTER):
                        split_k(b, u // 2 + 1, half, head)
                    if h == W_HIGH_AFTER:
                        split_w(b, u + 3)
                    if (u, h) in SPLIT_X_AFTER:
                        split_x(b + 1, SPLIT_X_AFTER.index((u, h)))

                for i in range(2):
                    split_w(0, i)
                for ct in range(CT):
                    split_x(0, ct, first=True)
                split_w(0, 2)
                act.wait_ge(wv_in_sem, 16 * (layer + 1))
                nc.scalar.activation(wv[:, 0, :, :], v[:, 0:CT, :], ACT.Copy).then_inc(wv_high, 1)
                act.wait_ge(prep_done, 2 * layer + 1)
                act.wait_ge(zeroed, 4)
                for which in range(5):
                    first_of(0, which)

                with act.Fori(0, B) as b:
                    split_max(b, 0)
                    for u in range(UNITS):
                        for h in range(STEPS):
                            exp_step(b, u, h)
                            if h == CONTEXT_AFTER and u > 0:
                                take_context(b, u - 1)
                            after_step(b, u, h)
                        if u + 1 < UNITS:
                            split_max(b, u + 1)
                    take_context(b, UNITS - 1)
                    for n in range(OUT_TILES + 2):
                        if n in FIRST_BEFORE:
                            first_of(b + 1, FIRST_BEFORE.index(n))
                        out_step(b, n)

        @block.vector
        def _(dve):
            for layer in range(LAYERS):
                def split_w(b, i, layer=layer):
                    pair, which = i // 2, 1 - i % 2
                    dve.wait_ge(w_high.sem, w_high.at(layer, b, i + 1))
                    nc.vector.scalar_tensor_tensor(
                        out=wqk[:, pair % 2, which, 1, :], in0=wqk_raw[:, :], scalar=1.0 if which else QUERY_SCALE[layer],
                        in1=wqk[:, pair % 2, which, 0, :].bitcast(F32), op0=ALU.mult, op1=ALU.subtract)\
                        .then_inc(w_low.sem, 1)

                def x_tile(b, ct, load, first, layer=layer):
                    if first:
                        dve.wait_ge(first_x_in[ct], 16 * (layer + 1))
                        return heads_out[:, ct, :]
                    dve.wait_ge(x_loaded[ct % 2].sem, x_loaded[ct % 2].at(layer, b, load + 1 - CT))
                    return x_in[:, ct % 2, :]

                def image_stats(b, ct, halves=(0, 1), first=False):
                    tile = x_tile(b, ct, ct // 2, first)
                    for i in halves:
                        op = nc.vector.bn_stats(bn[:, ct, 6 * i:6 * i + 6], tile[:, columns_of(i, HALF)])
                    if i == 1:
                        op.then_inc(bn_done.sem, 1)

                def group_deviation(b, layer=layer):
                    step = lambda k: dve.wait_ge(gn_step.sem, gn_step.at(layer, b, k))
                    dve.wait_ge(gn_mean_acc.sem, gn_mean_acc.at(layer, b, 1))
                    dve.wait_ge(gn_coef.sem, gn_coef.at(layer, b, 0))
                    nc.vector.tensor_reduce(g_mean[:, :], gen_ps[:, 0:CT * PARTS].rearrange("p (c g) -> p c g", g=PARTS),
                                            AX_X, ALU.add).then_inc(gn_step.sem, 1)
                    step(1)
                    for ct in range(CT):
                        op = nc.vector.tensor_scalar(g_dev[:, PARTS * ct:PARTS * ct + PARTS],
                                                     part_means[:, PARTS * ct:PARTS * ct + PARTS],
                                                     g_mean[:, ct:ct + 1], None, ALU.subtract)
                    op.then_inc(gn_step.sem, 1)
                    step(2)
                    nc.vector.tensor_tensor(g_sq[:, :], g_dev[:, :], g_dev[:, :], ALU.mult).then_inc(gn_step.sem, 1)
                    step(3)
                    nc.vector.scalar_tensor_tensor(out=g_exp[:, :], in0=part_squares, scalar=float(PARTS) / T,
                                                   in1=g_sq[:, :], op0=ALU.mult, op1=ALU.add).then_inc(gn_step.sem, 1)

                def group_variance(b, layer=layer):
                    dve.wait_ge(gn_var_acc.sem, gn_var_acc.at(layer, b, 1))
                    nc.vector.tensor_reduce(g_sum[:, :], gen_ps[:, 0:CT * PARTS].rearrange("p (c g) -> p c g", g=PARTS),
                                            AX_X, ALU.add).then_inc(gn_step.sem, 1)
                    dve.wait_ge(gn_step.sem, gn_step.at(layer, b, 5))
                    nc.vector.tensor_scalar(g_var[:, :], g_sum[:, :], EPS, None, ALU.add).then_inc(gn_step.sem, 1)

                def normalise(b, ct, layer=layer, first=False):
                    tile = x_tile(b, ct, 2 + ct // 2, first)
                    dve.wait_ge(gn_coef.sem, gn_coef.at(layer, b, 4))
                    nc.vector.tensor_scalar(tile, tile, g_scale[:, ct:ct + 1],
                                            g_shift[:, ct:ct + 1], ALU.mult, ALU.add).then_inc(x_norm.sem, 1)

                def split_x(b, ct, layer=layer, first=False):
                    tile = heads_out[:, ct, :] if first else x_in[:, ct % 2, :]
                    dve.wait_ge(x_high.sem, x_high.at(layer, b, ct + 1))
                    nc.vector.tensor_tensor(xn[:, 1, ct, :], tile, xn[:, 0, ct, :].bitcast(F32),
                                            ALU.subtract).then_inc(x_low.sem, 1)

                def split_k(b, pair, half, head):
                    own, ring, cs = OWN[head], pair % 2, columns_of(half, HALF)
                    dve.wait_ge(k_high.sem, k_high.at(layer, b, 4 * pair + 2 * half + head + 1))
                    nc.vector.scalar_tensor_tensor(
                        out=k_parts[OTHER[head], ring, head, cs], in0=k_ps[own, :],
                        scalar=bk[own, pair % PAIRS:pair % PAIRS + 1], in1=k_parts[own, ring, head, cs].bitcast(F32),
                        op0=ALU.add, op1=ALU.subtract).then_inc(k_low_done.sem, 1)

                def split_q(b, u, head):
                    own, ring, pair = OWN[head], u % 2, u // 2 % PAIRS
                    dve.wait_ge(q_high.sem, q_high.at(layer, b, 2 * u + head + 1))
                    nc.vector.scalar_tensor_tensor(
                        out=q_low[own, ring, head, :], in0=q_ps[own, :], scalar=bqs[own, pair:pair + 1],
                        in1=q_both[own, ring, head, :].bitcast(F32), op0=ALU.add, op1=ALU.subtract)\
                        .then_inc(q_low_done.sem, 1)

                def take_v(b, jt):
                    dve.wait_ge(v_acc.sem, v_acc.at(layer, b, jt + 1))
                    dve.wait_ge(pv_acc.sem, pv_acc.at(layer, b, 0))
                    nc.vector.tensor_tensor(v[:, jt, :], (q_ps, k_ps)[jt % 2][:, :], bias_rows[:, 0, :], ALU.add)\
                        .then_inc(v_done.sem, 1)

                def row_max(b, u, m):
                    half, it, head = m // MAX_HALF, m // 2 % QUERY_TILES, m % 2
                    dve.wait_ge(max_acc.sem, max_acc.at(layer, b, MAX_STEPS * u + m + 1))
                    if m == 0:
                        dve.wait_ge(max_both.sem, max_both.at(layer, b, u))
                    nc.vector.tensor_reduce(half_max[:, half, it, head:head + 1], max_banks[m % 3],
                                            AX_X, ALU.max, negate=True).then_inc(max_done.sem, 1)

                def both_halves(b, u):
                    dve.wait_ge(max_done.sem, max_done.at(layer, b, MAX_STEPS * (u + 1)))
                    dve.wait_ge(mt_acc.sem, mt_acc.at(layer, b, u))
                    for head in range(2):
                        col = MAX_ROWS[head][0]
                        op = nc.vector.tensor_tensor(neg_max[:, :, col], half_max[:, 0, :, head],
                                                     half_max[:, 1, :, head], ALU.min)
                    op.then_inc(max_both.sem, 1)

                def split_max(b, u):
                    for head in range(2):
                        dve.wait_ge(m_high.sem, m_high.at(layer, b, 2 * u + head + 1))
                        hi, lo = MAX_ROWS[head]
                        nc.vector.tensor_tensor(q_low[lo:lo + 1, u % 2, head, :], gen_ps[hi:hi + 1, :],
                                                q_low[hi:hi + 1, u % 2, head, :].bitcast(F32), ALU.subtract)\
                            .then_inc(m_low.sem, 1)

                def scale_context(b, u, part):
                    n = QUERY_TILES * u + part
                    if part == 0:
                        dve.wait_ge(l_acc.sem, l_acc.at(layer, b, u + 1))
                        dve.wait_ge(ctx_raw.sem, ctx_raw.at(layer, b, u + 1))
                    dve.wait_ge(ctx_done.sem, ctx_done.at(layer, b, max(n - 1, 0)))
                    nc.vector.reciprocal(inv_sum[:, part % 2, :], k_ps[:, columns_of(part)]).then_inc(inv_done.sem, 1)
                    dve.wait_ge(inv_done.sem, inv_done.at(layer, b, n + 1))
                    context = heads_out[:, u // 2, columns_of(u % 2 * QUERY_TILES + part)]
                    nc.vector.tensor_tensor(context, context, inv_sum[:, part % 2, :], ALU.mult).then_inc(ctx_done.sem, 1)

                def out_token(b, n):
                    r = n % 2
                    dve.wait_ge(o_acc.sem, o_acc.at(layer, b, n + 1))
                    dve.wait_ge(zt_acc.sem, zt_acc.at(layer, b, max(n - 1, 0)))
                    nc.vector.tensor_tensor(y_tok[:, r, :], max_ps[:, r, :], bias_rows[:, 1, :], ALU.add)\
                        .then_inc(y_done.sem, 1)
                    dve.wait_ge(y_done.sem, y_done.at(layer, b, n + 1))
                    nc.vector.bn_stats(ln_bn[:, r, :], y_tok[:, r, :]).then_inc(ln_stat.sem, 1)
                    dve.wait_ge(ln_stat.sem, ln_stat.at(layer, b, 4 * n + 1))
                    halves = ln_bn[:, r, :].rearrange("p (g k) -> p k g", k=3)
                    nc.vector.tensor_reduce(ln_sums[:, r, :], halves[:, 1:3, :], AX_X, ALU.add)
                    nc.vector.tensor_tensor(ln_diff[:, r, :], ln_bn[:, r, 1:2], ln_bn[:, r, 4:5], ALU.subtract)\
                        .then_inc(ln_stat.sem, 1)
                    dve.wait_ge(ln_stat.sem, ln_stat.at(layer, b, 4 * n + 2))
                    nc.vector.tensor_scalar(ln_mean[:, r, :], ln_sums[:, r, 0:1], 0.5, None, ALU.mult)
                    nc.vector.tensor_scalar(ln_within[:, r, :], ln_sums[:, r, 1:2], 1.0 / C, EPS, ALU.mult, ALU.add)
                    nc.vector.scalar_tensor_tensor(out=ln_between[:, r, :], in0=ln_diff[:, r, :], scalar=0.25,
                                                   in1=ln_diff[:, r, :], op0=ALU.mult, op1=ALU.mult)\
                        .then_inc(ln_stat.sem, 1)
                    dve.wait_ge(ln_stat.sem, ln_stat.at(layer, b, 4 * n + 3))
                    dve.wait_ge(ln_pow.sem, ln_pow.at(layer, b, max(n - 1, 0)))
                    nc.vector.tensor_tensor(ln_var[:, r, :], ln_within[:, r, :], ln_between[:, r, :], ALU.add)\
                        .then_inc(ln_stat.sem, 1)

                def norm_token(b, n):
                    r = n % 2
                    dve.wait_ge(ln_pow.sem, ln_pow.at(layer, b, n + 1))
                    nc.vector.tensor_scalar(y_tok[:, r, :], y_tok[:, r, :], ln_mean[:, r, :], ln_rstd[:, r, :],
                                            ALU.subtract, ALU.mult).then_inc(z_done.sem, 1)

                def add_residual(b, n):
                    r = n % 2
                    dve.wait_ge(res_in[r].sem, res_in[r].at(layer, b, n // 2 + 1))
                    if layer == 0:
                        dve.wait_ge(ln_done.sem, ln_done.at(layer, b, n + 1))
                        nc.vector.tensor_tensor(y_out[:, r, :], y_out[:, r, :], x_res[:, r, :], ALU.add)\
                            .then_inc(out_done.sem, 1)
                    else:
                        dve.wait_ge(o_acc.sem, o_acc.at(layer, b, n + 1))
                        dve.wait_ge(stored[r].sem, stored[r].at(layer, b, n // 2))
                        nc.vector.scalar_tensor_tensor(out=y_out[:, r, :], in0=max_ps[:, r, :],
                                                       scalar=cols[:, 4, n % CT:n % CT + 1], in1=x_res[:, r, :],
                                                       op0=ALU.add, op1=ALU.add).then_inc(out_done.sem, 1)

                def out_step(b, n):
                    if layer == 1:
                        if n < OUT_TILES:
                            add_residual(b, n)
                        return
                    if n < OUT_TILES:
                        out_token(b, n)
                    if 1 <= n <= OUT_TILES:
                        norm_token(b, n - 1)
                    if n >= 2:
                        add_residual(b, n - 2)

                def first_of(b, which):
                    if which >= 3:
                        take_v(b, which - 3)
                        return
                    for head in range(2):
                        if which == 1:
                            split_q(b, 0, head)
                        else:
                            split_k(b, 0, which // 2, head)

                def after_step(b, u, h):
                    if u + 1 < UNITS:
                        if h == Q_LOW_AFTER[0]:
                            split_q(b, u + 1, 0)
                        for m in max_steps_after(u, h):
                            row_max(b, u + 1, m)
                        if h == Q_LOW_AFTER[1]:
                            split_q(b, u + 1, 1)
                        if h == STEPS - 1:
                            both_halves(b, u + 1)
                    for half, head in k_splits(u, h, K_LOW_AFTER):
                        split_k(b, u // 2 + 1, half, head)
                    for unit, part in scales(u, h):
                        scale_context(b, unit, part)
                    if h == W_LOW_AFTER:
                        split_w(b, u + 3)
                    if u < CT and h in STATS_AFTER:
                        image_stats(b + 1, u, (STATS_AFTER.index(h),))
                    if (u, h) == (4, 1):
                        group_deviation(b + 1)
                    if (u, h) == (5, 1):
                        group_variance(b + 1)
                    if (u, h) in NORMALISE_AFTER:
                        normalise(b + 1, NORMALISE_AFTER.index((u, h)))
                    if (u, h) in LOW_X_AFTER:
                        split_x(b + 1, LOW_X_AFTER.index((u, h)))

                split_w(0, 0)
                for ct in range(CT):
                    image_stats(0, ct, first=True)
                group_deviation(0)
                dve.wait_ge(cols_in, 16 * (layer + 1))
                if layer:
                    dve.wait_ge(q_low_done.sem, q_low_done.at(layer, 0, 0))
                nc.vector.tensor_scalar(bqs[:, :], bq, QUERY_SCALE[layer], None, ALU.mult).then_inc(prep_done, 1)
                group_variance(0)
                split_w(0, 1)
                normalise(0, 0, first=True)
                for ct in range(1, CT):
                    normalise(0, ct, first=True)
                    split_x(0, ct - 1, first=True)
                split_x(0, CT - 1, first=True)
                split_w(0, 2)
                dve.wait_ge(wv_high, layer + 1)
                nc.vector.tensor_tensor(wv[:, 1, :, :], v[:, 0:CT, :], wv[:, 0, :, :].bitcast(F32), ALU.subtract)\
                    .then_inc(prep_done, 1)
                dve.wait_ge(zeroed, 4)
                dve.wait_ge(prep_done, 2 * layer + 1)
                dve.wait_ge(layer_in, 48 * (layer + 1))
                for which in range(5):
                    first_of(0, which)
                dve.wait_ge(prep_done, 2 * layer + 2)

                with dve.Fori(0, B) as b:
                    for m in range(MAX_STEPS):
                        row_max(b, 0, m)
                        if m == MAX_STEPS - 1:
                            both_halves(b, 0)
                        for chunk in v_chunks_after(m):
                            if chunk % CT == CT - 1:
                                take_v(b, 2 + chunk // CT)
                    split_max(b, 0)
                    for u in range(UNITS):
                        for h in range(STEPS):
                            after_step(b, u, h)
                        if u + 1 < UNITS:
                            split_max(b, u + 1)
                    for n in range(OUT_TILES + 2):
                        if n in FIRST_BEFORE:
                            first_of(b + 1, FIRST_BEFORE.index(n))
                        out_step(b, n)
                        for part in range(QUERY_TILES):
                            if n == SCALE_AFTER[3][part]:
                                scale_context(b, UNITS - 1, part)

        @block.gpsimd
        def _(pool):
            for counter in counts:
                pool.sem_inc(counter.sem, 1)
            nc.gpsimd.memset(k_ones.bitcast(F32), 0.0).then_inc(zeroed, 1)
            nc.gpsimd.memset(q_low[:, :, :, :].bitcast(F32), 0.0).then_inc(zeroed, 1)
            nc.gpsimd.memset(minus_half[:, :], -0.5)
            nc.gpsimd.memset(neg_max[:, :, :], 0.0).then_inc(zeroed, 1)
            pool.wait_ge(zeroed, 3)
            for head in range(2):
                for row in MAX_ROWS[head]:
                    op = nc.gpsimd.memset(k_ones[row:row + 1, :, head, :].bitcast(F32), 1.0)
            op.then_inc(zeroed, 1)
            pool.wait_ge(zeroed, 4)
            for layer in range(LAYERS):
                def coefficients(b, layer=layer):
                    step = lambda k: pool.wait_ge(gn_coef.sem, gn_coef.at(layer, b, k))
                    pool.wait_ge(gn_step.sem, gn_step.at(layer, b, 6))
                    pool.wait_ge(x_norm.sem, x_norm.at(layer, b, 0))
                    nc.gpsimd.tensor_tensor(g_rstd[:, :], g_var[:, :], minus_half[:, :], ALU.pow).then_inc(gn_coef.sem, 1)
                    step(1)
                    nc.gpsimd.tensor_tensor(g_scale[:, :], g_rstd[:, :], gamma, ALU.mult).then_inc(gn_coef.sem, 1)
                    step(2)
                    nc.gpsimd.tensor_tensor(g_tmp[:, :], g_mean[:, :], g_scale[:, :], ALU.mult).then_inc(gn_coef.sem, 1)
                    step(3)
                    nc.gpsimd.tensor_tensor(g_shift[:, :], beta, g_tmp[:, :], ALU.subtract).then_inc(gn_coef.sem, 1)

                def sum_step(b, u, h):
                    head, jt = h % 2, h // 2
                    total, new = e_sum[:, u % 2, head, :], e[:, h % RING, :]
                    if jt == 0:
                        return
                    pool.wait_ge(exp_done.sem, exp_done.at(layer, b, STEPS * u + h + 1))
                    if jt == 1:
                        pool.wait_ge(l_acc.sem, l_acc.at(layer, b, max(u - 1, 0)))
                        nc.gpsimd.tensor_tensor(total, e[:, head, :], new, ALU.add).then_inc(sum_done.sem, 1)
                    else:
                        pool.wait_ge(sum_done.sem, sum_done.at(layer, b, ADDS * u + 2 * (jt - 2) + head + 1))
                        nc.gpsimd.tensor_tensor(total, total, new, ALU.add).then_inc(sum_done.sem, 1)

                def out_step(b, n):
                    if layer == 0 and n < OUT_TILES:
                        r = n % 2
                        pool.wait_ge(ln_stat.sem, ln_stat.at(layer, b, 4 * n + 4))
                        pool.wait_ge(z_done.sem, z_done.at(layer, b, max(n - 1, 0)))
                        nc.gpsimd.tensor_tensor(ln_rstd[:, r, :], ln_var[:, r, :], minus_half[:, 0:1], ALU.pow)\
                            .then_inc(ln_pow.sem, 1)

                pool.wait_ge(cols_in, 16 * (layer + 1))
                coefficients(0)
                with pool.Fori(0, B) as b:
                    for u in range(UNITS):
                        for h in range(STEPS):
                            sum_step(b, u, h)
                            if (u, h) == (5, 4):
                                coefficients(b + 1)
                    for n in range(OUT_TILES):
                        out_step(b, n)


def kernel(**inputs):
    import numpy as np
    import concourse.bacc as bacc
    from concourse.bass_utils import run_bass_kernel_spmd

    def by_channel(vector):
        return vector.reshape(CT, P).T

    def transposed(w):
        return np.ascontiguousarray(w.T.reshape(CT, P, C).transpose(1, 0, 2))

    def by_pair(w):
        return w.reshape(PAIRS, P, CT, P).transpose(0, 3, 2, 1).reshape(PAIRS, P, CT * P)

    a = {name: np.asarray(value) for name, value in inputs.items()}
    x = a["x"].reshape(B, C, T)
    qkv_w, qkv_b = a["L1_conv_qkv_w"], a["L1_conv_qkv_b"]
    wq = [a["L0_conv_wq"], qkv_w[0:C]]
    wk = [a["L0_conv_wk"], qkv_w[C:2 * C]]
    wv = [a["L0_conv_wv"], qkv_w[2 * C:3 * C]]
    wo = [a["L0_conv_wo"], a["L1_conv_proj_w"]]
    per_channel = [
        [a["L0_conv_gn_gamma"], a["L0_conv_gn_beta"], a["L0_conv_bq"], a["L0_conv_bk"],
         a["L0_conv_ln_gamma"], a["L0_conv_ln_beta"]],
        [a["L1_conv_gn_scale"], a["L1_conv_gn_bias"], qkv_b[0:C], qkv_b[C:2 * C],
         a["L1_conv_proj_b"], a["L1_conv_proj_b"]],
    ]
    per_row = [[a["L0_conv_bv"], a["L0_conv_bo"]], [qkv_b[2 * C:3 * C], a["L1_conv_proj_b"]]]
    group = C // GROUPS
    constants = np.concatenate([
        np.eye(P, dtype=np.float32),
        np.kron(np.eye(P // group, dtype=np.float32), np.full((group, group), 1.0 / (group * PARTS), np.float32)),
        np.ones((P, D), np.float32),
    ], axis=1)

    arrays = {"in_x": x, "in_constants": constants}
    for layer in range(LAYERS):
        arrays[f"in_wqk{layer}"] = np.stack([by_pair(wq[layer]), by_pair(wk[layer])], axis=1)
        arrays[f"in_wv{layer}"] = transposed(wv[layer])
        arrays[f"in_wo{layer}"] = transposed(wo[layer])
        arrays[f"in_columns{layer}"] = np.stack([by_channel(c) for c in per_channel[layer]], axis=1)
        arrays[f"in_rows{layer}"] = np.stack(per_row[layer])
    arrays = {name: np.ascontiguousarray(value) for name, value in arrays.items()}

    nc = bacc.Bacc("TRN2", target_bir_lowering=False, num_devices=1)
    dram = {name: nc.dram_tensor(name, value.shape, F32, kind="ExternalInput").ap() for name, value in arrays.items()}
    middle = nc.dram_tensor("middle", [B, C, T], F32).ap()
    out = nc.dram_tensor("out", [B, C, T], F32, kind="ExternalOutput").ap()
    attention_blocks(nc, dram["in_x"], out, middle, [dram[f"in_wqk{i}"] for i in range(LAYERS)],
                     [dram[f"in_wv{i}"] for i in range(LAYERS)], [dram[f"in_wo{i}"] for i in range(LAYERS)],
                     [dram[f"in_columns{i}"] for i in range(LAYERS)], [dram[f"in_rows{i}"] for i in range(LAYERS)],
                     dram["in_constants"])
    result = run_bass_kernel_spmd(nc, [arrays], core_ids=[0])
    return result.results[0]["out"].reshape(B, C, 32, 32)
```
